# Optimizing a Trainium2 kernel written in Bass

```python
import numpy as np
import jax
import jax.numpy as jnp

def _softmax(x, axis=-1):
    return jax.nn.softmax(x, axis=axis)

def _gelu(x):
    return jax.nn.gelu(x, approximate=True)

def _silu(x):
    return jax.nn.silu(x)

def _sigmoid(x):
    return jax.nn.sigmoid(x)

def _layernorm(x, axis=-1, eps=1e-05):
    m = jnp.mean(x, axis=axis, keepdims=True)
    v = jnp.var(x, axis=axis, keepdims=True)
    return (x - m) / jnp.sqrt(v + eps)

def _scatter_add(tgt, idx, src, axis=0):
    return tgt.at[idx].add(src)

def _segment_sum(src, seg, n):
    return jax.ops.segment_sum(src, seg, n)
kernel_name = 'mk_gnn_preln_d2_gnn_r8_02c1ba'

def setup_inputs(seed: int=0):
    np.random.seed(seed)
    _w = jnp.asarray

    def _rec_inputs():
        import jax
        import jax.numpy as jnp
        _gk = jax.random.key(seed)
        x = -0.000202 + 1 * jax.random.normal(jax.random.fold_in(_gk, 1), (12500, 64), jnp.float32)
        src = jax.random.randint(jax.random.fold_in(_gk, 2), (200000,), 0, 12500, jnp.int32)
        dst = jax.random.randint(jax.random.fold_in(_gk, 3), (200000,), 0, 12500, jnp.int32)
        _o = jnp.argsort(dst, stable=True)
        src = src[_o]
        dst = dst[_o]
        return (x, src, dst)
    x, src, dst = _rec_inputs()

    def _L0_gnn_setup():
        import jax, jax.numpy as jnp
        import numpy as np
        N_NODES = 12500

        def gcn_conv(x, edge_index, W, b, num_nodes):
            src = jnp.concatenate([edge_index[0], jnp.arange(num_nodes, dtype=edge_index.dtype)])
            dst = jnp.concatenate([edge_index[1], jnp.arange(num_nodes, dtype=edge_index.dtype)])
            deg = jax.ops.segment_sum(jnp.ones_like(dst, dtype=x.dtype), dst, num_segments=num_nodes)
            dinv = jnp.where(deg > 0, jax.lax.rsqrt(deg), 0.0)
            norm = dinv[src] * dinv[dst]
            h = x @ W
            msg = h[src] * norm[:, None]
            out = jax.ops.segment_sum(msg, dst, num_segments=num_nodes)
            return out + b
        key = jax.random.key(seed)
        k1, k2, k3, k4, k5, k6 = jax.random.split(key, 6)
        d_in, d_hid, d_out = (64, 64, 64)
        x = jax.random.normal(k1, (N_NODES, d_in), dtype=jnp.float32)
        edge_index = jax.random.randint(k2, (2, 125000), 0, N_NODES, dtype=jnp.int64)
        W1 = jax.random.normal(k3, (d_in, d_hid), dtype=jnp.float32) / np.sqrt(d_in)
        b1 = jnp.zeros((d_hid,), dtype=jnp.float32)
        W2 = jax.random.normal(k4, (d_hid, d_out), dtype=jnp.float32) / np.sqrt(d_hid)
        b2 = jnp.zeros((d_out,), dtype=jnp.float32)
        return {'x': x, 'edge_index': edge_index, 'W1': W1, 'b1': b1, 'W2': W2, 'b2': b2}
    _L0_gnn_all = _L0_gnn_setup()
    _L0_gnn_in = {k: v for k, v in _L0_gnn_all.items() if k in ('W1', 'b1', 'W2', 'b2')}
    del _L0_gnn_all

    def _L1_gnn_setup():
        import jax, jax.numpy as jnp
        import numpy as np
        N_NODES = 6250
        N_EDGES = 100000
        D_FEAT = 64
        D_HID = 128
        D_OUT = 64
        key = jax.random.key(seed)
        k1, k2, k3, k4 = jax.random.split(key, 4)
        x = jax.random.normal(k1, (N_NODES, D_FEAT), dtype=jnp.float32)
        edge_index = jax.random.randint(k2, (2, N_EDGES), 0, N_NODES, dtype=jnp.int64)
        W1 = jax.random.normal(k3, (2 * D_FEAT, D_HID), dtype=jnp.float32) / np.sqrt(2 * D_FEAT)
        b1 = jnp.zeros((D_HID,), dtype=jnp.float32)
        W2 = jax.random.normal(k4, (D_HID, D_OUT), dtype=jnp.float32) / np.sqrt(D_HID)
        b2 = jnp.zeros((D_OUT,), dtype=jnp.float32)
        return {'x': x, 'edge_index': edge_index, 'W1': W1, 'b1': b1, 'W2': W2, 'b2': b2}
    _L1_gnn_all = _L1_gnn_setup()
    _L1_gnn_in = {k: v for k, v in _L1_gnn_all.items() if k in ('W1', 'b1', 'W2', 'b2')}
    del _L1_gnn_all
    return {'x': x, 'src': src, 'dst': dst, 'L0_gnn_W1': _L0_gnn_in['W1'], 'L0_gnn_b1': _L0_gnn_in['b1'], 'L0_gnn_W2': _L0_gnn_in['W2'], 'L0_gnn_b2': _L0_gnn_in['b2'], 'L1_gnn_W1': _L1_gnn_in['W1'], 'L1_gnn_b1': _L1_gnn_in['b1'], 'L1_gnn_W2': _L1_gnn_in['W2'], 'L1_gnn_b2': _L1_gnn_in['b2']}

def reference(x, src, dst, L0_gnn_W1, L0_gnn_b1, L0_gnn_W2, L0_gnn_b2, L1_gnn_W1, L1_gnn_b1, L1_gnn_W2, L1_gnn_b2):
    import jax
    import jax.numpy as jnp

    def _L0_gnn_ref(x, edge_index, W1, b1, W2, b2):
        import jax, jax.numpy as jnp
        import numpy as np
        N_NODES = 12500

        def gcn_conv(x, edge_index, W, b, num_nodes):
            src = jnp.concatenate([edge_index[0], jnp.arange(num_nodes, dtype=edge_index.dtype)])
            dst = jnp.concatenate([edge_index[1], jnp.arange(num_nodes, dtype=edge_index.dtype)])
            deg = jax.ops.segment_sum(jnp.ones_like(dst, dtype=x.dtype), dst, num_segments=num_nodes)
            dinv = jnp.where(deg > 0, jax.lax.rsqrt(deg), 0.0)
            norm = dinv[src] * dinv[dst]
            h = x @ W
            msg = h[src] * norm[:, None]
            out = jax.ops.segment_sum(msg, dst, num_segments=num_nodes)
            return out + b
        n = x.shape[0]
        h = jax.nn.relu(gcn_conv(x, edge_index, W1, b1, n))
        out = jax.nn.relu(gcn_conv(h, edge_index, W2, b2, n))
        return out

    def _L1_gnn_ref(x, edge_index, W1, b1, W2, b2):
        import jax, jax.numpy as jnp
        import numpy as np
        N_NODES = 6250
        N_EDGES = 100000
        D_FEAT = 64
        D_HID = 128
        D_OUT = 64
        n = x.shape[0]
        loops = jnp.arange(n, dtype=edge_index.dtype)
        src = jnp.concatenate([edge_index[0], loops])
        dst = jnp.concatenate([edge_index[1], loops])
        edge_features = jnp.concatenate([x[src], x[dst]], axis=-1)
        h = jax.nn.relu(edge_features @ W1 + b1)
        edge_out = h @ W2 + b2
        agg = jax.ops.segment_sum(edge_out, dst, num_segments=n)
        counts = jax.ops.segment_sum(jnp.ones_like(dst, dtype=edge_out.dtype), dst, num_segments=n)
        return agg / jnp.clip(counts, 1.0)[:, None]
    edge_index = jnp.stack([src, dst])
    h = jnp.maximum(_layernorm(x, axis=-1), 0.0)
    x = x + _L0_gnn_ref(h, edge_index, L0_gnn_W1, L0_gnn_b1, L0_gnn_W2, L0_gnn_b2)
    h = jnp.maximum(_layernorm(x, axis=-1), 0.0)
    x = x + _L1_gnn_ref(h, edge_index, L1_gnn_W1, L1_gnn_b1, L1_gnn_W2, L1_gnn_b2)
    return x

_drawn_inputs = setup_inputs


def setup_inputs(seed=0):
    import zlib

    import numpy as np

    out = dict(_drawn_inputs(seed))
    spreads = {'L0_gnn_b1': (0.0, 0.1),
     'L0_gnn_b2': (0.0, 0.1),
     'L1_gnn_b1': (0.0, 0.1),
     'L1_gnn_b2': (0.0, 0.1)}
    factors = {}
    for name, (base, spread) in spreads.items():
        noise = np.random.default_rng([zlib.crc32(name.encode()), seed]).standard_normal(out[name].shape)
        drawn = base * np.exp(spread * noise) if base else spread * noise
        out[name] = jnp.asarray(drawn.astype(out[name].dtype))
    for name, factor in factors.items():
        out[name] = (out[name] * factor).astype(out[name].dtype)
    return out
```

```python
from contextlib import ExitStack

import concourse.bass as bass
from concourse import mybir

F32 = mybir.dt.float32
BF16 = mybir.dt.bfloat16
I32 = mybir.dt.int32
ALU = mybir.AluOpType
ACT = mybir.ActivationFunctionType
AX_X = mybir.AxisListType.X

P = 128
EPS = 1e-5
W = 128
U = 8
WU = W // U
GT = 8
GE = GT * P
SLOTS = 8
CB = 4
CN = CB * P
DG = 4
DT = DG * GT
HG = DG // 2
PIECE = 5
LAG = 7
EARLY = 8
CONVS = ("conv1", "conv2")
PASSES = ("deg", "conv1", "conv2", "edge")


def gnn_program(nc, x, src, dst, w1, b1, w2, b2, ew1, eb1, ew2, eb2, out):
    N, D = x.shape
    E = src.shape[0]
    H = ew1.shape[1]
    CHUNKS = -(-N // CN)
    NB = CHUNKS * CB
    NP = NB * P
    G = -(-E // GE)
    R = G // 2
    RE = 2 * GE
    FULL = E // RE
    LEFT = E - FULL * RE
    LASTG = LEFT - GE
    LAST_TILES = -(-LASTG // P)
    EDGE_LOADS = 2 + (FULL % 16 > 0) + -(-(RE - LEFT) // LASTG)
    MAIN = (G - SLOTS) // SLOTS * SLOTS
    DSTEPS = G // DG
    FAR = -(-N // W)
    BASE_MAX = (NP - W) // U
    STORES = dict(conv1=CHUNKS // PIECE, conv2=CHUNKS)
    assert D == 64 and H == 128 and G % 2 == 0 and R <= P and FULL == R - 1 and GE < LEFT < RE
    assert CHUNKS % 2 == 1 and CHUNKS % PIECE == 0 and NP >= N + W and G % DG == 0 and DSTEPS % 2 == 1 and 2 * DSTEPS < NB
    assert CB * H == 512 and MAIN + SLOTS < G and PIECE <= LAG <= PIECE + 3

    u_tab = {p: nc.dram_tensor(f"{p}_table", (NP, D), F32, kind="Internal").ap() for p in CONVS}
    a_tab = nc.dram_tensor("source_table", (NP, H), F32, kind="Internal").ap()
    b_tab = nc.dram_tensor("target_table", (NP, H), F32, kind="Internal").ap()
    rel_row_b = nc.dram_tensor("relative_targets_bf16", (G, GE), BF16, kind="Internal").ap()
    rel_row_f = nc.dram_tensor("relative_targets", (G, GE), F32, kind="Internal").ap()
    base_row = nc.dram_tensor("group_bases", (G,), I32, kind="Internal").ap()
    extra_row = nc.dram_tensor("group_extra_windows", (G,), F32, kind="Internal").ap()

    def tiles(g):
        return LAST_TILES if isinstance(g, int) and g == G - 1 else GT

    def uses(g, s, ring):
        return g // ring if isinstance(g, int) else (g - s % ring) // ring

    with ExitStack() as ctx:
        def sb(name, shape, dt=F32):
            return ctx.enter_context(nc.sbuf_tensor(name, shape, dt))

        def sem(name):
            return ctx.enter_context(nc.semaphore(name))

        x_sb = sb("x_sb", [P, NB, D])
        t_sb = sb("t_sb", [P, NB, D])
        acc = sb("acc", [P, NP])
        gath = sb("gath", [P, SLOTS, GT, H])
        onehot = sb("onehot", [P, 2, GT, W])
        onehot_t = sb("onehot_t", [P, 2, GE])
        hidden = sb("hidden", [P, 2, GT, H])
        src_col = sb("src_col", [P, (G + SLOTS + 2) * GT], I32)
        rel_col = sb("rel_col", [P, G * GT])
        idx = sb("idx", [P, SLOTS, GT], I32)
        rel_bc = sb("rel_bc", [P, 2, GE], BF16)
        b_win = sb("b_win", [P, 2, H])
        base_sb = sb("base_sb", [1, G], I32)
        sweep_tab = sb("sweep_tab", [1, G, 2], I32)
        extra_sb = sb("extra_sb", [1, 4, G])
        flat = gath[:, :, :, :].rearrange("p a b c -> p (a b c)")
        dst_i, src_i = flat[:, 0:RE].bitcast(I32), flat[:, RE:2 * RE].bitcast(I32)
        rel_rows, src_f = flat[:, 2 * RE:3 * RE], flat[:, 3 * RE:4 * RE]
        rel_i, lo_i, hi_i = (flat[:, k * RE:k * RE + G * GT].bitcast(I32) for k in (0, 1, 3))
        LW = G * GT + 2 * DT
        hflat = hidden[:, :, :, :].rearrange("p a b c -> p (a b c)")
        lo_b, hi_b = hflat[:, 0:LW // 2].bitcast(BF16), hflat[:, LW // 2:LW].bitcast(BF16)
        deg = onehot_t[:, :, :].rearrange("p a b -> p (a b)")[0:U, 0:NP // U]
        deg_pool = flat[0:U, 2 * RE:2 * RE + NP // U]
        stats = onehot[:, :, :, :].rearrange("p a b c -> p (a b c)")[:, 0:NB * 6].rearrange(
            "p (b s) -> p b s", s=6)
        a_rows = onehot_t[:, :, :].rearrange("p k (c f) -> p k c f", f=H)[:, :, 0:CB, :]
        b_rows = hidden[:, :, 0:CB, :]
        sweep_rel = hidden[:, 1, :, :].rearrange("p c f -> p (c f)")
        ident = sb("ident", [P, P])
        iota_w = sb("iota_w", [P, W])
        pidx = sb("pidx", [P, 1])
        lo_ref, hi_ref = sb("lo_ref", [P, U, DT], BF16), sb("hi_ref", [P, WU, DT], BF16)
        lo_hot, hi_hot = sb("lo_hot", [P, 2, U, DT], BF16), sb("hi_hot", [P, 2, WU, DT], BF16)
        far_w, far_u = sb("far_w", [P, FAR + 2]), sb("far_u", [P, FAR + 2])
        select = sb("select", [U, WU, P])
        deg_stage = sb("deg_stage", [U, 2, HG * WU])
        far_col, far_hi = sb("far_col", [P, GT]), sb("far_hi", [P, GT], BF16)
        rel_rows_b = sb("rel_rows_b", [P, RE], BF16)
        gmin, gmax, base_f = (sb(n, [P, 2]) for n in ("gmin", "gmax", "base_f"))
        gmin_i, base_u, base_i, extra_i = (sb(n, [P, 2], I32) for n in ("gmin_i", "base_u", "base_i", "extra_i"))
        extra_f = sb("extra_f", [P, 2])
        cnt, root, dinv, rcnt, total, spread, var, std, rstd, shift = (sb(n, [P, NB]) for n in (
            "cnt", "root", "dinv", "rcnt", "total", "spread", "var", "std", "rstd", "shift"))
        w1_sb, w2_sb = sb("w1_sb", [D, D]), sb("w2_sb", [D, D])
        wab_sb, wself_sb = sb("wab_sb", [D, 2, H]), sb("wself_sb", [D, H])
        ew2_sb = sb("ew2_sb", [H, D])
        b1_bc, b2_bc, eb2_bc = sb("b1_bc", [P, D]), sb("b2_bc", [P, D]), sb("eb2_bc", [P, D])
        eb1_bc, eb1_col = sb("eb1_bc", [P, H]), sb("eb1_col", [P, 1])

        ps_e = ctx.enter_context(nc.psum_tensor("ps_e", [P, 2, 2 * 512], F32))
        ps_a = ctx.enter_context(nc.psum_tensor("ps_a", [P, 2, 512], F32))
        ps_z = ctx.enter_context(nc.psum_tensor("ps_z", [P, 2, 512], F32))

        dst_loaded, src_loaded, x_zeroed, x_loaded, weights_loaded = (sem(n) for n in (
            "dst_loaded", "src_loaded", "x_zeroed", "x_loaded", "weights_loaded"))
        consts_made, made_step, deg_zeroed = sem("consts_made"), sem("made_step"), sem("deg_zeroed")
        rel_ready, src_ready, rel_turned, src_turned, src_col_ready = (sem(n) for n in (
            "rel_ready", "src_ready", "rel_turned", "src_turned", "src_col_ready"))
        rel_b_ready, extra_ready = sem("rel_b_ready"), sem("extra_ready")
        base_stored, rel_stored, base_loaded, extra_loaded = (sem(n) for n in (
            "base_stored", "rel_stored", "base_loaded", "extra_loaded"))
        dve_step = sem("dve_step")
        sweep_tab_ready = sem("sweep_tab_ready")
        deg_hot_ready, deg_summed, deg_added, deg_turned, cnt_ready, root_ready = (sem(n) for n in (
            "deg_hot_ready", "deg_summed", "deg_added", "deg_turned", "cnt_ready", "root_ready"))
        var_ready, std_ready, shift_ready, x_normed = (sem(n) for n in (
            "var_ready", "std_ready", "shift_ready", "x_normed"))
        onehot_ready = {p: sem(f"onehot_ready_{p}") for p in PASSES[1:]}
        summed = {p: sem(f"summed_{p}") for p in PASSES[1:]}
        added = {p: sem(f"added_{p}") for p in PASSES[1:]}
        slot_ready = {p: sem(f"slot_ready_{p}") for p in PASSES[1:]}
        gathered = {p: [sem(f"gathered_{p}_{s}") for s in range(SLOTS)] for p in PASSES[1:]}
        gather_turn = sem("gather_turn")
        pass_done = {p: sem(f"pass_done_{p}") for p in PASSES}
        rows_ready = {p: sem(f"rows_ready_{p}") for p in PASSES[1:]}
        rows_turned = {p: sem(f"rows_turned_{p}") for p in PASSES[1:]}
        acc_started = {p: sem(f"acc_started_{p}") for p in PASSES[1:]}
        table_stored = {p: sem(f"table_stored_{p}") for p in CONVS}
        product_ready = {p: sem(f"product_ready_{p}") for p in PASSES[1:]}
        scaled = {p: sem(f"scaled_{p}") for p in CONVS}
        x_updated, x_biased = sem("x_updated"), sem("x_biased")
        deg_pool_zeroed, deg_staged = sem("deg_pool_zeroed"), sem("deg_staged")
        deg_added_pool, deg_summed_pool = sem("deg_added_pool"), sem("deg_summed_pool")
        wself_ready = sem("wself_ready")
        h_copied, self_ready = sem("h_copied"), sem("self_ready")
        a_ready, a_copied, b_ready, b_copied = (sem(n) for n in ("a_ready", "a_copied", "b_ready", "b_copied"))
        a_stored = [sem(f"a_stored_{k}") for k in range(2)]
        b_stored = [sem(f"b_stored_{k}") for k in range(2)]
        window_loaded = [sem(f"window_loaded_{k}") for k in range(2)]
        onehot_t_ready, expanded, messages_added, hidden_ready = (sem(n) for n in (
            "onehot_t_ready", "expanded", "messages_added", "hidden_ready"))
        out_ready, out_stored = sem("out_ready"), sem("out_stored")
        sw = {p: {n: sem(f"sweep_{n}_{p}") for n in (
            ("rel", "hot", "summed", "added") if p == "deg" else
            ("staged", "gathered", "rel", "hot", "summed", "added") if p in CONVS else
            ("staged", "gathered", "rel", "hot", "summed", "added",
             "loaded", "hot_t", "expanded", "messages", "hidden"))} for p in PASSES}

        def stored_chunks(sems, chunks):
            return [(sems[k], 16 * len(range(k, chunks, 2))) for k in range(2)]

        def bcast(small, c, n=CB):
            return small[:, bass.ds(c, n)].unsqueeze(2).to_broadcast([P, n, D])

        def for_groups(eng, body):
            with eng.Fori(0, MAIN, SLOTS) as i:
                for s in range(SLOTS):
                    body(i + s, s)
            for g in range(MAIN, G):
                body(g, g % SLOTS)

        def for_chunks(eng, body):
            with eng.Fori(0, CHUNKS - 1, 2) as i:
                for k in range(2):
                    body(i + k, k)
            body(CHUNKS - 1, 0)

        def sweep(eng, body):
            eng.wait_ge(sweep_tab_ready, 1)
            many = eng.value_load(sweep_tab[0:1, G - 1, 1:2], min_val=0, max_val=G * FAR)
            with eng.If(many > 0):
                with eng.Fori(0, G) as g:
                    first = eng.value_load(sweep_tab[0:1, bass.ds(g, 1), 0:1].rearrange("p a b -> p (a b)"),
                                           min_val=0, max_val=G * FAR)
                    end = eng.value_load(sweep_tab[0:1, bass.ds(g, 1), 1:2].rearrange("p a b -> p (a b)"),
                                         min_val=0, max_val=G * FAR)
                    with eng.If(first < end):
                        with eng.Fori(first, end) as n:
                            body(g, n, within(n - first + 1, 1, FAR))

        def within(value, low, high):
            return nc.s_assert_within(value, low, high, skip_runtime_bounds_check_because=
                                      "the table holds windows up to the group's greatest target")

        def load_base(eng, g):
            return eng.value_load(base_sb[0:1, bass.ds(g, 1)], min_val=0, max_val=BASE_MAX)

        def far_base(eng, g, j):
            return within(load_base(eng, g) + j * WU, 0, BASE_MAX)

        block = ctx.enter_context(nc.Block())

        @block.sync
        def _(sp):
            for staged, edges, loaded in ((dst_i, dst, dst_loaded), (src_i, src, src_loaded)):
                lead = FULL // 16 * 16
                sp.dma_start(staged[0:lead, :], edges[0:lead * RE].rearrange("(p e) -> p e", e=RE)
                             ).then_inc(loaded, 16)
                if lead < FULL:
                    sp.dma_start(staged[lead:FULL, :], edges[lead * RE:FULL * RE].rearrange("(p e) -> p e", e=RE)
                                 ).then_inc(loaded, 16)
                at, start, n = 0, FULL * RE, LEFT
                while at < RE:
                    sp.dma_start(staged[FULL:R, at:at + n], edges[start:start + n].rearrange("(p e) -> p e", p=1)
                                 ).then_inc(loaded, 16)
                    at, start, n = at + n, E - LASTG, min(LASTG, RE - at - n)
            sp.dma_start(x_sb[:, 0:N // P, :], x[0:N // P * P, :].rearrange("(b p) d -> p b d", p=P)
                         ).then_inc(x_loaded, 16)
            sp.wait_ge(x_zeroed, 1)
            sp.dma_start(x_sb[0:N % P, N // P, :], x[N // P * P:N, :]).then_inc(x_loaded, 16)
            sp.wait_ge(rel_ready, 1)
            sp.dma_start(base_row.rearrange("(r k) -> r k", k=2), base_u[0:R, :]).then_inc(base_stored, 16)
            sp.wait_ge(base_stored, 16)
            sp.dma_start(base_sb[:, :], base_row.rearrange("(a g) -> a g", a=1)).then_inc(base_loaded, 16)
            sp.dma_start(rel_row_f.rearrange("(r k) e -> r (k e)", k=2), rel_rows[0:R, :]).then_inc(rel_stored, 16)
            sp.wait_ge(extra_ready, 1)
            sp.dma_start(extra_row.rearrange("(r k) -> r k", k=2), extra_f[0:R, :]).then_inc(base_stored, 16)
            sp.wait_ge(base_stored, 32)
            sp.dma_start(extra_sb[0:1, 0, :], extra_row.rearrange("(a g) -> a g", a=1)).then_inc(extra_loaded, 16)
            sp.wait_ge(rel_b_ready, 1)
            sp.dma_start(rel_row_b.rearrange("(r k) e -> r (k e)", k=2), rel_rows_b[0:R, :]).then_inc(rel_stored, 16)

            for c in range(0, CHUNKS, PIECE):
                sp.wait_ge(rows_ready["conv1"], c + PIECE)
                sp.dma_start(u_tab["conv1"][c * CN:(c + PIECE) * CN, :].rearrange("(b p) d -> p b d", p=P),
                             t_sb[:, c * CB:(c + PIECE) * CB, :]).then_inc(table_stored["conv1"], 16)

            def store_table(c, k):
                sp.wait_ge(rows_ready["conv2"], c + 1)
                sp.dma_start(u_tab["conv2"][bass.ds(c * CN, CN), :].rearrange("(b p) d -> p b d", p=P),
                             t_sb[:, bass.ds(c * CB, CB), :]).then_inc(table_stored["conv2"], 16)
            for_chunks(sp, store_table)

            def store_chunk(table, rows, copied, stored):
                def body(c, k):
                    sp.wait_ge(copied, c + 3)
                    sp.dma_start(table[bass.ds(c * CN, CN), :].rearrange("(b p) f -> p b f", p=P),
                                 rows[:, k]).then_inc(stored[k], 16)
                for_chunks(sp, body)
            store_chunk(a_tab, a_rows, a_copied, a_stored)
            store_chunk(b_tab, b_rows, b_copied, b_stored)
            for what, value in stored_chunks(b_stored, CHUNKS) + [(rel_stored, 32)]:
                sp.wait_ge(what, value)

            def load_window(g, s):
                k = s % 2
                sp.wait_ge(expanded, g + 1)
                sp.dma_start(b_win[:, k, :], b_tab[bass.ds(load_base(sp, g) * U, W), :]
                             ).then_inc(window_loaded[k], 16)
                sp.dma_start(rel_bc[:, k, :], rel_row_b[bass.ds(g, 1), :].to_broadcast([P, GE])
                             ).then_inc(window_loaded[k], 16)
            for_groups(sp, load_window)

            def sweep_load(g, n, j):
                sp.wait_ge(sw["edge"]["added"], n + 1)
                sp.dma_start(b_win[:, 0, :], b_tab[bass.ds(far_base(sp, g, j) * U, W), :]
                             ).then_inc(sw["edge"]["loaded"], 16)
                sp.dma_start(sweep_rel, rel_row_f[bass.ds(g, 1), :].to_broadcast([P, GE])
                             ).then_inc(sw["edge"]["loaded"], 16)
            sweep(sp, sweep_load)

            with sp.Fori(0, N // CN) as c:
                sp.wait_ge(out_ready, c + 1)
                sp.dma_start(out[bass.ds(c * CN, CN), :].rearrange("(b p) d -> p b d", p=P),
                             t_sb[:, bass.ds(c * CB, CB), :]).then_inc(out_stored, 16)
            sp.wait_ge(out_ready, CHUNKS)
            last_blocks = range(N // CN * CB, -(-N // P))
            for b in last_blocks:
                rows = min(P, N - b * P)
                sp.dma_start(out[b * P:b * P + rows, :], t_sb[0:rows, b, :]).then_inc(out_stored, 16)
            sp.wait_ge(out_stored, 16 * (N // CN + len(last_blocks)))

        @block.gpsimd
        def _(pool):
            exact = dict(allow_small_or_imprecise_dtypes=True)
            pool.memset(ident[:, :], 0.0).then_inc(made_step, 1)
            pool.memset(select[:, :, :], 0.0).then_inc(made_step, 1)
            pool.memset(x_sb[:, N // P:NB, :], 0.0).then_inc(x_zeroed, 1)
            pool.wait_ge(made_step, 2)
            pool.affine_select(out=ident[:, :], in_=ident[:, :], compare_op=ALU.not_equal, fill=1.0,
                               base=0, pattern=[[-1, P]], channel_multiplier=1).then_inc(consts_made, 1)
            pool.iota(lo_ref[:, :, :], pattern=[[1, U], [0, DT]], base=0, channel_multiplier=0,
                      **exact).then_inc(consts_made, 1)
            pool.iota(hi_ref[:, :, :], pattern=[[1, WU], [0, DT]], base=0, channel_multiplier=0,
                      **exact).then_inc(consts_made, 1)
            pool.memset(deg, 0.0).then_inc(deg_zeroed, 1)
            pool.iota(iota_w[:, :], pattern=[[1, W]], base=0, channel_multiplier=0, **exact).then_inc(consts_made, 1)
            pool.iota(pidx[:, :], pattern=[[1, 1]], base=0, channel_multiplier=1, **exact).then_inc(consts_made, 1)
            pool.iota(far_w[:, :], pattern=[[W, FAR + 2]], base=0, channel_multiplier=0,
                      **exact).then_inc(consts_made, 1)
            pool.iota(far_u[:, :], pattern=[[WU, FAR + 2]], base=0, channel_multiplier=0,
                      **exact).then_inc(consts_made, 1)
            pool.affine_select(out=select[:, :, :], in_=select[:, :, :], compare_op=ALU.not_equal, fill=1.0,
                               base=0, pattern=[[U, WU], [-1, P]], channel_multiplier=1).then_inc(consts_made, 1)

            def gather_group(table, width, s, n, done):
                for c in range(n):
                    pool.indirect_dma_start(
                        out=gath[:, s, c, 0:width], out_offset=None, in_=table,
                        in_offset=bass.IndirectOffsetOnAxis(ap=idx[:, s, c:c + 1], axis=0)).then_inc(done, 16)

            def gather_pass(p, table, width):
                def body(g, s):
                    pool.wait_ge(slot_ready[p], g + 1)
                    pool.sem_inc(gather_turn, 1)
                    gather_group(table, width, s, tiles(g), gathered[p][s])
                for_groups(pool, body)

                def sweep_gather(g, n, j):
                    pool.wait_ge(sw[p]["staged"], n + 1)
                    pool.sem_inc(gather_turn, 1)
                    gather_group(table, width, 0, GT, sw[p]["gathered"])
                sweep(pool, sweep_gather)

            pool.wait_ge(rel_turned, 1)
            pool.wait_ge(rel_stored, 32)
            pool.memset(deg_pool, 0.0).then_inc(deg_pool_zeroed, 1)
            pool.wait_ge(deg_pool_zeroed, 1)
            pool.wait_ge(base_loaded, 16)
            pool.sem_inc(deg_added_pool, HG + 1)

            def deg_step(q, k):
                pool.wait_ge(deg_staged, q + 3)
                for j in range(HG):
                    pool.wait_ge(deg_added_pool, q * HG + j + HG + 1)
                    window = deg_pool[:, bass.ds(load_base(pool, q * DG + HG + j), WU)]
                    pool.tensor_tensor(window, deg_stage[:, k, j * WU:(j + 1) * WU], window, ALU.add
                                       ).then_inc(deg_added_pool, 1)
            with pool.Fori(0, DSTEPS - 1, 2) as i:
                for k in range(2):
                    deg_step(i + k, k)
            deg_step(DSTEPS - 1, 0)

            for p in CONVS:
                pool.wait_ge(table_stored[p], 16 * STORES[p])
                gather_pass(p, u_tab[p], D)
            for what, value in stored_chunks(a_stored, CHUNKS):
                pool.wait_ge(what, value)
            gather_pass("edge", a_tab, H)

        @block.vector
        def _(dve):
            steps = [0]

            def link(ins):
                steps[0] += 1
                ins.then_inc(dve_step, 1)
                dve.wait_ge(dve_step, steps[0])

            def halves(ap):
                return [ap[0:R, k * GE:(k + 1) * GE] for k in range(2)]

            dve.wait_ge(dst_loaded, 16 * EDGE_LOADS)
            link(dve.tensor_reduce(gmin[0:R, :], dst_i[0:R, :].rearrange("p (k e) -> p k e", k=2), AX_X, ALU.min))
            link(dve.tensor_copy(gmin_i[0:R, :], gmin[0:R, :]))
            link(dve.tensor_scalar(base_u[0:R, :], gmin_i[0:R, :], 3, None, ALU.arith_shift_right))
            link(dve.tensor_scalar(base_i[0:R, :], base_u[0:R, :], 3, None, ALU.logical_shift_left))
            link(dve.tensor_copy(base_f[0:R, :], base_i[0:R, :]))
            for k in range(2):
                last = dve.tensor_scalar(halves(rel_rows)[k], halves(dst_i)[k], base_f[0:R, k:k + 1], None,
                                         ALU.subtract)
            last.then_inc(rel_ready, 1)
            link(dve.tensor_reduce(gmax[0:R, :], dst_i[0:R, :].rearrange("p (k e) -> p k e", k=2), AX_X, ALU.max))
            link(dve.tensor_tensor(gmax[0:R, :], gmax[0:R, :], base_f[0:R, :], ALU.subtract))
            link(dve.tensor_copy(extra_i[0:R, :], gmax[0:R, :]))
            link(dve.tensor_scalar(extra_i[0:R, :], extra_i[0:R, :], 7, None, ALU.arith_shift_right))
            dve.tensor_copy(extra_f[0:R, :], extra_i[0:R, :]).then_inc(extra_ready, 1)
            dve.tensor_copy(rel_rows_b[0:R, :], rel_rows[0:R, :]).then_inc(rel_b_ready, 1)

            def row_stats(b):
                return dve.bn_stats(stats[:, b, :], x_sb[:, b, :])

            def finish_stats(b, n, turn):
                s = slice(b, b + n)
                dve.tensor_tensor(total[:, s], stats[:, s, 1], stats[:, s, 4], ALU.add)
                dve.tensor_tensor(spread[:, s], stats[:, s, 1], stats[:, s, 4], ALU.subtract)
                link(dve.tensor_tensor(var[:, s], stats[:, s, 2], stats[:, s, 5], ALU.add))
                dve.tensor_tensor(spread[:, s], spread[:, s], spread[:, s], ALU.mult)
                link(dve.tensor_scalar(var[:, s], var[:, s], 1.0 / D, EPS, ALU.mult, ALU.add))
                dve.scalar_tensor_tensor(out=var[:, s], in0=spread[:, s], scalar=0.25, in1=var[:, s],
                                         op0=ALU.mult, op1=ALU.add).then_inc(var_ready, 1)
                dve.wait_ge(std_ready, turn)
                link(dve.reciprocal(rstd[:, s], std[:, s]))
                dve.scalar_tensor_tensor(out=shift[:, s], in0=total[:, s], scalar=-0.5, in1=rstd[:, s],
                                         op0=ALU.mult, op1=ALU.mult).then_inc(shift_ready, 1)

            dve.wait_ge(rel_turned, 1)
            for j in range(4):
                last = dve.tensor_copy(
                    rel_col[:, :].rearrange("p (r kc) -> p kc r", kc=2 * GT)[:, 4 * j:4 * j + 4, :],
                    ps_e[:, j // 2, (j % 2) * 512:(j % 2) * 512 + 4 * R].rearrange("p (a r) -> p a r", a=4))
            link(last)
            full, part = E // P, E % P
            link(dve.memset(rel_col[part:P, full:full + 1], -1.0))
            link(dve.memset(rel_col[:, full + 1:G * GT], -1.0))
            link(dve.tensor_copy(rel_i, rel_col[:, :]))
            dve.wait_ge(src_turned, 1)
            dve.tensor_scalar(lo_i, rel_i, U - 1, None, ALU.bitwise_and)
            link(dve.tensor_scalar(hi_i, rel_i, 3, None, ALU.arith_shift_right))
            dve.tensor_copy(lo_b[:, 0:G * GT], lo_i)
            link(dve.tensor_copy(hi_b[:, 0:G * GT], hi_i))

            def deg_hot(q, k):
                dve.tensor_tensor(lo_hot[:, k], lo_ref[:, :, :],
                                  lo_b[:, bass.ds(q * DT, DT)].unsqueeze(1).to_broadcast([P, U, DT]), ALU.is_equal)
                dve.tensor_tensor(hi_hot[:, k], hi_ref[:, :, :],
                                  hi_b[:, bass.ds(q * DT, DT)].unsqueeze(1).to_broadcast([P, WU, DT]),
                                  ALU.is_equal).then_inc(deg_hot_ready, 1)

            def deg_step(q, k):
                if not (isinstance(q, int) and q + 1 >= DSTEPS):
                    dve.wait_ge(deg_staged, q + 2)
                    deg_hot(q + 1, (k + 1) % 2)
                dve.wait_ge(deg_summed, q + 1)
                for j in range(HG):
                    dve.wait_ge(deg_added, q * HG + j + HG + 1)
                    window = deg[:, bass.ds(load_base(dve, q * DG + j), WU)]
                    dve.tensor_tensor(window, ps_a[0:U, k, j * WU:(j + 1) * WU], window, ALU.add
                                      ).then_inc(deg_added, 1)

            dve.wait_ge(consts_made, 8)
            dve.wait_ge(deg_zeroed, 1)
            dve.wait_ge(base_loaded, 16)
            dve.sem_inc(deg_added, HG + 1)
            deg_hot(0, 0)
            dve.wait_ge(x_loaded, 32)
            for b in range(NB):
                last = row_stats(b)
            link(last)
            finish_stats(0, NB, 1)
            with dve.Fori(0, DSTEPS - 1, 2) as i:
                for k in range(2):
                    deg_step(i + k, k)
            deg_step(DSTEPS - 1, 0)
            dve.wait_ge(deg_added, DSTEPS * HG + HG + 1)
            dve.wait_ge(deg_added_pool, DSTEPS * HG + HG + 1)
            link(dve.tensor_tensor(deg, deg, deg_pool, ALU.add))
            dve.wait_ge(extra_loaded, 16)
            link(dve.memset(extra_sb[0:1, 1, :], 0.0))
            link(dve.tensor_tensor_scan(extra_sb[0:1, 2, :], extra_sb[0:1, 0, :], extra_sb[0:1, 1, :], 0.0,
                                        ALU.add, ALU.add))
            link(dve.tensor_tensor(extra_sb[0:1, 3, :], extra_sb[0:1, 2, :], extra_sb[0:1, 0, :], ALU.subtract))
            link(dve.tensor_copy(sweep_tab[0:1, :, 1], extra_sb[0:1, 2, :]))
            dve.tensor_copy(sweep_tab[0:1, :, 0], extra_sb[0:1, 3, :]).then_inc(sweep_tab_ready, 1)

            def sweep_deg(g, n, j):
                s = sw["deg"]
                dve.tensor_copy(far_col[:, :], hi_i[:, bass.ds(g * GT, GT)]).then_inc(s["rel"], 1)
                dve.wait_ge(s["rel"], n * 2 + 1)
                dve.tensor_scalar(far_hi[:, :], far_col[:, :], far_u[:, bass.ds(j, 1)], None, ALU.subtract
                                  ).then_inc(s["rel"], 1)
                dve.wait_ge(s["rel"], n * 2 + 2)
                dve.tensor_tensor(lo_hot[:, 0, :, 0:GT], lo_ref[:, :, 0:GT],
                                  lo_b[:, bass.ds(g * GT, GT)].unsqueeze(1).to_broadcast([P, U, GT]), ALU.is_equal)
                dve.tensor_tensor(hi_hot[:, 0, :, 0:GT], hi_ref[:, :, 0:GT],
                                  far_hi[:, :].unsqueeze(1).to_broadcast([P, WU, GT]), ALU.is_equal
                                  ).then_inc(s["hot"], 1)
                dve.wait_ge(s["summed"], n + 1)
                window = deg[:, bass.ds(far_base(dve, g, j), WU)]
                dve.tensor_tensor(window, ps_a[0:U, 0, 0:WU], window, ALU.add).then_inc(s["added"], 1)
                dve.wait_ge(s["added"], n + 1)
            sweep(dve, sweep_deg)
            dve.sem_inc(pass_done["deg"], 1)

            dve.wait_ge(deg_turned, 1)
            dve.tensor_scalar(cnt[:, :], ps_z[:, 0, 0:NB], 1.0, None, ALU.add).then_inc(cnt_ready, 1)
            dve.wait_ge(root_ready, 1)
            link(dve.reciprocal(dinv[:, :], root[:, :]))
            dve.reciprocal(rcnt[:, :], cnt[:, :])
            dve.wait_ge(x_normed, DSTEPS + 1)
            for c in range(0, CHUNKS, PIECE):
                rows = t_sb[:, c * CB:(c + PIECE) * CB, :]
                dve.tensor_tensor(rows, rows, bcast(dinv, c * CB, PIECE * CB), ALU.mult
                                  ).then_inc(rows_ready["conv1"], PIECE)

            def make_onehot(p, g, k):
                n = tiles(g)
                dve.tensor_tensor(onehot[:, k, 0:n, :], iota_w[:, :].unsqueeze(1).to_broadcast([P, n, W]),
                                  rel_col[:, bass.ds(g * GT, n)].unsqueeze(2).to_broadcast([P, n, W]),
                                  ALU.is_equal).then_inc(onehot_ready[p], 1)

            def add_window(p, g, k, rows):
                dve.wait_ge(summed[p], g + 1)
                dve.wait_ge(added[p], g + 2)
                window = acc[0:rows, bass.ds(load_base(dve, g) * U, W)]
                dve.tensor_tensor(window, ps_a[0:rows, k, 0:W], window, ALU.add).then_inc(added[p], 1)

            def stage(p, g, s):
                dve.tensor_copy(idx[:, s, :], src_col[:, bass.ds(g * GT, GT)]).then_inc(slot_ready[p], 1)

            def stage_next(p, g, s):
                if not isinstance(g, int) or g + SLOTS < G:
                    stage(p, g + SLOTS, s)

            def sweep_sums(p, rows, messages=None):
                s = sw[p]
                dve.wait_ge(added[p], G + 2)
                dve.sem_inc(s["added"], 1)

                def body(g, n, j):
                    dve.tensor_copy(idx[:, 0, :], src_col[:, bass.ds(g * GT, GT)]).then_inc(s["staged"], 1)
                    dve.tensor_scalar(far_col[:, :], rel_col[:, bass.ds(g * GT, GT)], far_w[:, bass.ds(j, 1)],
                                      None, ALU.subtract).then_inc(s["rel"], 1)
                    dve.wait_ge(s["rel"], n + 1)
                    dve.tensor_tensor(onehot[:, 0], iota_w[:, :].unsqueeze(1).to_broadcast([P, GT, W]),
                                      far_col[:, :].unsqueeze(2).to_broadcast([P, GT, W]), ALU.is_equal
                                      ).then_inc(s["hot"], 1)
                    if messages:
                        messages(g, n, j)
                    dve.wait_ge(s["summed"], n + 1)
                    window = acc[0:rows, bass.ds(far_base(dve, g, j) * U, W)]
                    dve.tensor_tensor(window, ps_a[0:rows, 0, 0:W], window, ALU.add).then_inc(s["added"], 1)
                    dve.wait_ge(s["added"], n + 2)
                sweep(dve, body)
                dve.sem_inc(pass_done[p], 1)

            def conv_sums(p):
                for s in range(SLOTS):
                    stage(p, s, s)
                make_onehot(p, 0, 0)
                dve.wait_ge(acc_started[p], 2 + CHUNKS)
                dve.sem_inc(added[p], 2)

                def body(g, s):
                    if not (isinstance(g, int) and g + 1 >= G):
                        make_onehot(p, g + 1, (s + 1) % 2)
                    add_window(p, g, s % 2, D)
                    stage_next(p, g, s)
                for_groups(dve, body)
                sweep_sums(p, D)

            def scale_rows(p, c, k, factor, other):
                dve.wait_ge(product_ready[p], c + 1)
                for j in range(CB):
                    b = bass.ds(c * CB + j, 1)
                    last = dve.scalar_tensor_tensor(
                        out=t_sb[:, b, :].rearrange("p a d -> p (a d)"), in0=ps_z[:, k, j * D:(j + 1) * D],
                        scalar=factor[:, b], in1=other(b), op0=ALU.mult, op1=ALU.add)
                last.then_inc(scaled[p], 1)
                return t_sb[:, bass.ds(c * CB, CB), :]

            dve.wait_ge(src_col_ready, 1)
            conv_sums("conv1")

            dve.wait_ge(weights_loaded, 16 * 9)
            dve.wait_ge(table_stored["conv1"], 16 * STORES["conv1"])
            dve.sem_inc(scaled["conv1"], 2)

            def second_table(c, k):
                rows = scale_rows("conv1", c, k, dinv, lambda b: b1_bc[:, :])
                dve.wait_ge(scaled["conv1"], c + 3)
                dve.scalar_tensor_tensor(out=rows, in0=rows, scalar=0.0, in1=bcast(dinv, c * CB),
                                         op0=ALU.max, op1=ALU.mult).then_inc(rows_ready["conv2"], 1)
            for_chunks(dve, second_table)
            conv_sums("conv2")

            dve.wait_ge(table_stored["conv2"], 16 * CHUNKS)
            dve.sem_inc(scaled["conv2"], 2)
            for c in range(CHUNKS):
                rows = scale_rows("conv2", c, c % 2, dinv, lambda b: b2_bc[:, :])
                dve.wait_ge(scaled["conv2"], c + 3)
                xs = x_sb[:, c * CB:(c + 1) * CB, :]
                dve.scalar_tensor_tensor(out=xs, in0=rows, scalar=0.0, in1=xs, op0=ALU.max, op1=ALU.add
                                         ).then_inc(x_updated, 1)
                dve.wait_ge(x_updated, c + 1)
                for b in range(c * CB, (c + 1) * CB):
                    last = row_stats(b)
                if c % PIECE == PIECE - 1:
                    link(last)
                    finish_stats((c - PIECE + 1) * CB, PIECE * CB, c // PIECE + 2)
            dve.tensor_tensor(wself_sb[:, :], wab_sb[:, 0, :], wab_sb[:, 1, :], ALU.add).then_inc(wself_ready, 1)
            for s in range(SLOTS):
                stage("edge", s, s)
            make_onehot("edge", 0, 0)
            make_onehot("edge", 1, 1)
            dve.sem_inc(b_copied, 2)
            for c in range(CHUNKS):
                k = c % 2
                dve.wait_ge(b_ready, c + 1)
                if c >= 2:
                    dve.wait_ge(b_stored[k], 16 * (c // 2))
                dve.tensor_tensor(b_rows[:, k], ps_z[:, k, :].rearrange("p (b f) -> p b f", f=H),
                                  eb1_bc[:, :].unsqueeze(1).to_broadcast([P, CB, H]), ALU.add
                                  ).then_inc(b_copied, 1)

            def make_onehot_t(g, s):
                k = s % 2
                dve.wait_ge(window_loaded[k], (uses(g, s, 2) + 1) * 32)
                dve.tensor_scalar(onehot_t[:, k, :], rel_bc[:, k, :], pidx[:, 0:1], None,
                                  ALU.is_equal).then_inc(onehot_t_ready, 1)

            def gathered_count(g, s):
                if isinstance(g, int):
                    return 16 * (GT * (g // SLOTS) + tiles(g))
                return uses(g, s, SLOTS) * (16 * GT) + 16 * GT

            def add_messages(g, s):
                k, n = s % 2, tiles(g)
                dve.wait_ge(expanded, g + 3)
                dve.wait_ge(gathered["edge"][s], gathered_count(g, s))
                dve.tensor_tensor(hidden[:, k, 0:n, :], ps_e[:, k, 0:n * H].rearrange("p (c f) -> p c f", f=H),
                                  gath[:, s, 0:n, :], ALU.add).then_inc(messages_added, 1)
                stage_next("edge", g, s)

            for what, value in stored_chunks(a_stored, CHUNKS) + stored_chunks(b_stored, CHUNKS):
                dve.wait_ge(what, value)
            dve.sem_inc(messages_added, 1)
            for g in range(2):
                make_onehot_t(g, g)
            for g in range(2):
                add_messages(g, g)
            dve.wait_ge(rows_ready["edge"], CHUNKS)
            dve.tensor_tensor(x_sb[:, :, :], x_sb[:, :, :],
                              eb2_bc[:, :].unsqueeze(1).to_broadcast([P, NB, D]), ALU.add).then_inc(x_biased, 1)
            dve.wait_ge(acc_started["edge"], 2 + CHUNKS)
            dve.sem_inc(added["edge"], 2)

            def edge_group(g, s):
                two_ahead = not isinstance(g, int) or g + 2 < G
                if two_ahead:
                    make_onehot_t(g + 2, (s + 2) % SLOTS)
                add_window("edge", g, s % 2, H)
                if two_ahead:
                    make_onehot("edge", g + 2, s % 2)
                    add_messages(g + 2, (s + 2) % SLOTS)
            for_groups(dve, edge_group)

            def sweep_messages(g, n, j):
                s = sw["edge"]
                dve.wait_ge(s["loaded"], n * 32 + 32)
                dve.tensor_scalar(onehot_t[:, 0, :], sweep_rel, far_w[:, bass.ds(j, 1)], pidx[:, 0:1],
                                  ALU.subtract, ALU.is_equal).then_inc(s["hot_t"], 1)
                dve.wait_ge(s["expanded"], n + 1)
                dve.wait_ge(s["gathered"], n * (16 * GT) + 16 * GT)
                dve.tensor_tensor(hidden[:, 0], ps_e[:, 0, :].rearrange("p (c f) -> p c f", f=H),
                                  gath[:, 0], ALU.add).then_inc(s["messages"], 1)
            sweep_sums("edge", H, sweep_messages)

            dve.wait_ge(x_biased, 1)

            def finish(c, k):
                dve.wait_ge(product_ready["edge"], c + 1)
                for j in range(CB):
                    b = bass.ds(c * CB + j, 1)
                    last = dve.scalar_tensor_tensor(
                        out=t_sb[:, b, :].rearrange("p a d -> p (a d)"), in0=ps_z[:, k, j * D:(j + 1) * D],
                        scalar=rcnt[:, b], in1=x_sb[:, b, :].rearrange("p a d -> p (a d)"),
                        op0=ALU.mult, op1=ALU.add)
                last.then_inc(out_ready, 1)
            for_chunks(dve, finish)

        @block.scalar
        def _(act):
            for t, d in ((w1_sb[:, :], w1), (w2_sb[:, :], w2), (ew2_sb[:, :], ew2),
                         (wab_sb[:, :, :], ew1.rearrange("(k d) f -> d k f", k=2)),
                         (b1_bc[:, :], b1.partition_broadcast(P)), (b2_bc[:, :], b2.partition_broadcast(P)),
                         (eb2_bc[:, :], eb2.partition_broadcast(P)), (eb1_bc[:, :], eb1.partition_broadcast(P)),
                         (eb1_col[:, :], eb1.rearrange("(p a) -> p a", a=1))):
                act.dma_start(t, d).then_inc(weights_loaded, 16)
            act.wait_ge(src_loaded, 16 * EDGE_LOADS)
            act.activation(src_f[0:R, :], src_i[0:R, :], ACT.Copy).then_inc(src_ready, 1)
            act.wait_ge(src_turned, 1)
            for j in range(4):
                ps = (ps_a, ps_z)[j // 2]
                last = act.activation(
                    src_col[:, 0:G * GT].rearrange("p (r kc) -> p kc r", kc=2 * GT)[:, 4 * j:4 * j + 4, :],
                    ps[:, j % 2, 0:4 * R].rearrange("p (a r) -> p a r", a=4), ACT.Copy)
            last.then_inc(src_col_ready, 1)

            def take_root(b, n, turn):
                act.wait_ge(var_ready, turn)
                act.activation(std[:, b:b + n], var[:, b:b + n], ACT.Sqrt).then_inc(std_ready, 1)

            def normalise(b):
                b = bass.ds(b, 1)
                return act.activation(t_sb[:, b, :].rearrange("p a d -> p (a d)"),
                                      x_sb[:, b, :].rearrange("p a d -> p (a d)"), ACT.Relu,
                                      scale=rstd[:, b], bias=shift[:, b])

            take_root(0, NB, 1)
            act.wait_ge(shift_ready, 1)
            act.sem_inc(deg_staged, 2)

            def deg_step(q, k):
                for j in range(2):
                    last = normalise(q * 2 + j)
                last.then_inc(x_normed, 1)
                act.wait_ge(deg_summed_pool, q + 1)
                act.wait_ge(deg_added_pool, q * HG + 1)
                act.activation(deg_stage[:, k, :], ps_z[0:U, k, 0:HG * WU], ACT.Copy).then_inc(deg_staged, 1)
            with act.Fori(0, DSTEPS - 1, 2) as i:
                for k in range(2):
                    deg_step(i + k, k)
            deg_step(DSTEPS - 1, 0)
            for b in range(2 * DSTEPS, NB):
                last = normalise(b)
            last.then_inc(x_normed, 1)
            act.wait_ge(cnt_ready, 1)
            act.activation(root[:, :], cnt[:, :], ACT.Sqrt).then_inc(root_ready, 1)

            for p in CONVS:
                act.sem_inc(acc_started[p], 2)

                def start_acc(c, k):
                    act.wait_ge(rows_turned[p], c + 1)
                    act.activation(acc[0:D, bass.ds(c * CN, CN)], ps_e[0:D, k, 0:CN], ACT.Copy
                                   ).then_inc(acc_started[p], 1)
                for_chunks(act, start_acc)

            act.sem_inc(h_copied, 2)
            act.sem_inc(a_copied, 2)

            def copy_h(c):
                act.wait_ge(rows_turned["edge"], c + 1)
                act.activation(acc[0:D, c * CN:(c + 1) * CN], ps_e[0:D, c % 2, 0:CN], ACT.Copy
                               ).then_inc(h_copied, 1)

            def copy_a(c):
                act.wait_ge(a_ready, c + 1)
                if c >= 2:
                    act.wait_ge(a_stored[c % 2], 16 * (c // 2))
                act.activation(a_rows[:, c % 2], ps_a[:, c % 2, :].rearrange("p (b f) -> p b f", f=H), ACT.Copy
                               ).then_inc(a_copied, 1)

            for c in range(CHUNKS + 2):
                if c < CHUNKS:
                    if c % PIECE == 0:
                        take_root(c * CB, PIECE * CB, c // PIECE + 2)
                        act.wait_ge(shift_ready, c // PIECE + 2)
                    for b in range(c * CB, (c + 1) * CB):
                        last = normalise(b)
                    last.then_inc(rows_ready["edge"], 1)
                if 1 <= c <= CHUNKS:
                    copy_h(c - 1)
                if c >= 2:
                    copy_a(c - 2)
            act.sem_inc(acc_started["edge"], 2)
            for c in range(CHUNKS):
                act.wait_ge(self_ready, c + 1)
                act.activation(acc[:, c * CN:(c + 1) * CN], ps_z[:, c % 2, :], ACT.Relu,
                               bias=eb1_col[:, 0:1]).then_inc(acc_started["edge"], 1)

            def relu_messages(g, s):
                act.wait_ge(messages_added, g + 2)
                rows = hidden[:, s % 2, 0:tiles(g), :]
                act.activation(rows, rows, ACT.Relu).then_inc(hidden_ready, 1)
            for_groups(act, relu_messages)

            def sweep_relu(g, n, j):
                act.wait_ge(sw["edge"]["messages"], n + 1)
                act.activation(hidden[:, 0], hidden[:, 0], ACT.Relu).then_inc(sw["edge"]["hidden"], 1)
            sweep(act, sweep_relu)

        @block.tensor
        def _(pe):
            pe.wait_ge(consts_made, 1)
            for rows, ready, turned, banks in (
                    (rel_rows, rel_ready, rel_turned, [ps_e[:, 0, 0:512], ps_e[:, 0, 512:], ps_e[:, 1, 0:512],
                                                       ps_e[:, 1, 512:]]),
                    (src_f, src_ready, src_turned, [ps_a[:, 0, :], ps_a[:, 1, :], ps_z[:, 0, :], ps_z[:, 1, :]])):
                pe.wait_ge(ready, 1)
                for j in range(2 * GT):
                    last = pe.transpose(banks[j // 4][:, j % 4 * R:(j % 4 + 1) * R],
                                        rows[0:R, j * P:(j + 1) * P], ident[0:R, 0:R])
                last.then_inc(turned, 1)

            def deg_step(q, k):
                pe.wait_ge(deg_hot_ready, q + 1)
                for half, (ps, emptied, per_step, done) in enumerate(((ps_a, deg_added, HG, deg_summed),
                                                                      (ps_z, deg_staged, 1, deg_summed_pool))):
                    pe.wait_ge(emptied, q * per_step + 1)
                    for t in range(HG * GT):
                        g, c = t // GT, t % GT
                        at = half * HG * GT + t
                        last = pe.matmul(ps[0:U, k, g * WU:(g + 1) * WU], lo_hot[:, k, :, at],
                                         hi_hot[:, k, :, at], start=(c == 0), stop=(c == GT - 1))
                    last.then_inc(done, 1)

            pe.wait_ge(src_col_ready, 1)
            with pe.Fori(0, DSTEPS - 1, 2) as i:
                for k in range(2):
                    deg_step(i + k, k)
            deg_step(DSTEPS - 1, 0)

            def sweep_deg(g, n, j):
                pe.wait_ge(sw["deg"]["hot"], n + 1)
                for c in range(GT):
                    last = pe.matmul(ps_a[0:U, 0, 0:WU], lo_hot[:, 0, :, c], hi_hot[:, 0, :, c],
                                     start=(c == 0), stop=(c == GT - 1))
                last.then_inc(sw["deg"]["summed"], 1)
            sweep(pe, sweep_deg)
            pe.wait_ge(pass_done["deg"], 1)
            pe.wait_ge(consts_made, 8)
            for q in range(WU):
                last = pe.matmul(ps_z[:, 0, 0:NB], select[:, q, :],
                                 deg.rearrange("l (b q) -> l q b", q=WU)[:, q, :],
                                 start=(q == 0), stop=(q == WU - 1))
            last.then_inc(deg_turned, 1)

            def turn_rows(p, c, k):
                for j in range(CB):
                    last = pe.transpose(ps_e[0:D, k, j * P:(j + 1) * P], t_sb[:, c * CB + j, :], ident[:, :])
                last.then_inc(rows_turned[p], 1)

            def multiply(p, c, rows, weights):
                if p in CONVS:
                    pe.wait_ge(scaled[p], c + 1)
                elif c >= 2:
                    pe.wait_ge(out_ready, c - 1)
                for j in range(CB):
                    last = pe.matmul(ps_z[:, c % 2, j * D:(j + 1) * D],
                                     acc[0:rows, c * CN + j * P:c * CN + (j + 1) * P], weights,
                                     start=True, stop=True)
                last.then_inc(product_ready[p], 1)

            def own_terms(p, c):
                pe.wait_ge(rows_ready[p], c + 1)
                pe.wait_ge(acc_started[p], c + 1)
                turn_rows(p, c, c % 2)

            def sum_group(p, g, s, weights, waits):
                k, n = s % 2, tiles(g)
                for what, value in waits:
                    pe.wait_ge(what, value)
                pe.wait_ge(onehot_ready[p], g + 1)
                pe.wait_ge(added[p], g + 1)
                for c in range(n):
                    lhs = weights(c)
                    last = pe.matmul(ps_a[0:lhs.shape[1], k, 0:W], lhs, onehot[:, k, c, :],
                                     start=(c == 0), stop=(c == n - 1))
                last.then_inc(summed[p], 1)

            def sweep_sum(p, n, weights):
                pe.wait_ge(sw[p]["hot"], n + 1)
                for c in range(GT):
                    lhs = weights(c)
                    last = pe.matmul(ps_a[0:lhs.shape[1], 0, 0:W], lhs, onehot[:, 0, c, :],
                                     start=(c == 0), stop=(c == GT - 1))
                last.then_inc(sw[p]["summed"], 1)

            def conv_sums(p):
                def body(g, s):
                    count = (16 * (GT * (g // SLOTS) + tiles(g)) if isinstance(g, int)
                             else uses(g, s, SLOTS) * (16 * GT) + 16 * GT)
                    sum_group(p, g, s, lambda c: gath[:, s, c, 0:D], [(gathered[p][s], count)])
                for_groups(pe, body)

                def sweep_conv(g, n, j):
                    pe.wait_ge(sw[p]["gathered"], n * (16 * GT) + 16 * GT)
                    sweep_sum(p, n, lambda c: gath[:, 0, c, 0:D])
                sweep(pe, sweep_conv)
                pe.wait_ge(pass_done[p], 1)

            for c in range(CHUNKS):
                own_terms("conv1", c)
            conv_sums("conv1")
            pe.wait_ge(weights_loaded, 16 * 9)
            for c in range(CHUNKS):
                multiply("conv1", c, D, w1_sb[:, :])
            for c in range(CHUNKS):
                own_terms("conv2", c)
            conv_sums("conv2")

            def turn_chunk(c):
                pe.wait_ge(rows_ready["edge"], c + 1)
                pe.wait_ge(h_copied, c + 1)
                turn_rows("edge", c, c % 2)

            def table_products(c, ps, side, done):
                for j in range(CB):
                    last = pe.matmul(ps[:, c % 2, j * H:(j + 1) * H],
                                     acc[0:D, c * CN + j * P:c * CN + (j + 1) * P], wab_sb[:, side, :],
                                     start=True, stop=True)
                last.then_inc(done, 1)

            for c in range(CHUNKS + LAG + 1):
                if c < CHUNKS:
                    multiply("conv2", c, D, w2_sb[:, :])
                if LAG <= c < CHUNKS + LAG:
                    turn_chunk(c - LAG)
                if c > LAG:
                    pe.wait_ge(h_copied, c - LAG + 2)
                    pe.wait_ge(a_copied, c - LAG)
                    table_products(c - LAG - 1, ps_a, 0, a_ready)
            pe.wait_ge(scaled["conv2"], CHUNKS + 2)
            for c in range(CHUNKS):
                pe.wait_ge(b_copied, c + 1)
                table_products(c, ps_z, 1, b_ready)
            pe.sem_inc(expanded, 2)

            def expand(g, s):
                k = s % 2
                pe.wait_ge(onehot_t_ready, g + 1)
                pe.wait_ge(window_loaded[k], (uses(g, s, 2) + 1) * 32)
                if not (isinstance(g, int) and g == 0):
                    pe.wait_ge(messages_added, g)
                for c in range(tiles(g)):
                    last = pe.matmul(ps_e[:, k, c * H:(c + 1) * H], onehot_t[:, k, c * P:(c + 1) * P],
                                     b_win[:, k, :], start=True, stop=True)
                last.then_inc(expanded, 1)

            pe.wait_ge(b_copied, CHUNKS + 2)
            pe.wait_ge(wself_ready, 1)
            for c in range(CHUNKS):
                if c in (EARLY, EARLY + 1):
                    expand(c - EARLY, c - EARLY)
                pe.wait_ge(acc_started["edge"], c + 1)
                pe.matmul(ps_z[:, c % 2, :], wself_sb[:, :], acc[0:D, c * CN:(c + 1) * CN],
                          start=True, stop=True).then_inc(self_ready, 1)
            pe.wait_ge(acc_started["edge"], CHUNKS + 2)

            def edge_group(g, s):
                sum_group("edge", g, s, lambda c: hidden[:, s % 2, c, :], [(hidden_ready, g + 1)])
                if not (isinstance(g, int) and g + 2 >= G):
                    expand(g + 2, (s + 2) % SLOTS)
            for_groups(pe, edge_group)

            def sweep_edge(g, n, j):
                s = sw["edge"]
                pe.wait_ge(s["loaded"], n * 32 + 32)
                pe.wait_ge(s["hot_t"], n + 1)
                for c in range(GT):
                    last = pe.matmul(ps_e[:, 0, c * H:(c + 1) * H], onehot_t[:, 0, c * P:(c + 1) * P],
                                     b_win[:, 0, :], start=True, stop=True)
                last.then_inc(s["expanded"], 1)
                pe.wait_ge(s["hidden"], n + 1)
                sweep_sum("edge", n, lambda c: hidden[:, 0, c, :])
            sweep(pe, sweep_edge)
            pe.wait_ge(pass_done["edge"], 1)
            for c in range(CHUNKS):
                multiply("edge", c, H, ew2_sb[:, :])


_INS = ["x", "src", "dst", "L0_gnn_W1", "L0_gnn_b1", "L0_gnn_W2", "L0_gnn_b2",
        "L1_gnn_W1", "L1_gnn_b1", "L1_gnn_W2", "L1_gnn_b2"]


def kernel(**inputs):
    import numpy as np
    import concourse.bacc as bacc
    from concourse.bass_utils import run_bass_kernel_spmd

    nc = bacc.Bacc("TRN2", target_bir_lowering=False, num_devices=1)
    arrays, args = {}, []
    for name in _INS:
        a = np.ascontiguousarray(inputs[name])
        arrays[f"in_{name}"] = a
        args.append(nc.dram_tensor(f"in_{name}", a.shape, mybir.dt.from_np(a.dtype), kind="ExternalInput").ap())
    out = nc.dram_tensor("out_0", inputs["x"].shape, F32, kind="ExternalOutput").ap()
    gnn_program(nc, *args, out)
    r = run_bass_kernel_spmd(nc, [arrays], core_ids=[0])
    return r.results[0]["out_0"]
```

```python
from contextlib import ExitStack

import concourse.bass as bass
from concourse import mybir

F32 = mybir.dt.float32
BF16 = mybir.dt.bfloat16
I32 = mybir.dt.int32
ALU = mybir.AluOpType
ACT = mybir.ActivationFunctionType
AX_X = mybir.AxisListType.X

P = 128
EPS = 1e-5
W = 128
U = 8
WU = W // U
GT = 8
GE = GT * P
SLOTS = 8
BEHIND = 2
CB = 4
CN = CB * P
DG = 4
DT = DG * GT
HG = DG // 2
TABLE_PIECE = 5
EARLY = 8
CONVS = ("conv1", "conv2")
PASSES = ("deg", "conv1", "conv2", "edge")


def gnn_program(nc, x, src, dst, w1, b1, w2, b2, ew1, eb1, ew2, eb2, out):
    N, D = x.shape
    E = src.shape[0]
    H = ew1.shape[1]
    CHUNKS = -(-N // CN)
    NB = CHUNKS * CB
    NP = NB * P
    G = -(-E // GE)
    R = G // 2
    RE = 2 * GE
    FULL = E // RE
    LEFT = E - FULL * RE
    LASTG = LEFT - GE
    LAST_TILES = -(-LASTG // P)
    EDGE_LOADS = 2 + (FULL % 16 > 0) + -(-(RE - LEFT) // LASTG)
    MAIN = (G - SLOTS) // SLOTS * SLOTS
    ROUNDS = MAIN // SLOTS
    AHEAD = G // SLOTS - BEHIND
    DSTEPS = G // DG
    X_PIECES = [(b, b + NB // 4) for b in range(0, NB, NB // 4)]
    FAR = -(-N // W)
    BASE_MAX = (NP - W) // U
    STORES = dict(conv1=CHUNKS // TABLE_PIECE, conv2=CHUNKS)
    assert D == 64 and H == 128 and G % 2 == 0 and R <= P and FULL == R - 1 and GE < LEFT < RE
    assert CHUNKS % 2 == 1 and CHUNKS % TABLE_PIECE == 0 and NP >= N + W and G % DG == 0
    assert DSTEPS % 2 == 1 and 2 * DSTEPS < NB
    assert AHEAD < N // CN and CB * H == 512 and MAIN + SLOTS < G

    u_tab = {p: nc.dram_tensor(f"{p}_table", (NP, D), F32, kind="Internal").ap() for p in CONVS}
    a_tab = nc.dram_tensor("source_table", (NP, H), F32, kind="Internal").ap()
    b_tab = nc.dram_tensor("target_table", (NP, H), F32, kind="Internal").ap()
    rel_row_b = nc.dram_tensor("relative_targets_bf16", (G, GE), BF16, kind="Internal").ap()
    rel_row_f = nc.dram_tensor("relative_targets", (G, GE), F32, kind="Internal").ap()
    base_row = nc.dram_tensor("group_bases", (G,), I32, kind="Internal").ap()
    extra_row = nc.dram_tensor("group_extra_windows", (G,), F32, kind="Internal").ap()

    def tiles(g):
        return LAST_TILES if isinstance(g, int) and g == G - 1 else GT

    def uses(g, s, ring):
        return g // ring if isinstance(g, int) else (g - s % ring) // ring

    with ExitStack() as ctx:
        def sb(name, shape, dt=F32):
            return ctx.enter_context(nc.sbuf_tensor(name, shape, dt))

        def sem(name):
            return ctx.enter_context(nc.semaphore(name))

        x_sb = sb("x_sb", [P, NB, D])
        t_sb = sb("t_sb", [P, NB, D])
        acc = sb("acc", [P, NP])
        gath = sb("gath", [P, SLOTS, GT, H])
        onehot = sb("onehot", [P, 2, GT, W])
        onehot_t = sb("onehot_t", [P, 2, GE])
        hidden = sb("hidden", [P, 2, GT, H])
        src_col = sb("src_col", [P, (G + SLOTS + 2) * GT], I32)
        rel_col = sb("rel_col", [P, G * GT])
        idx = sb("idx", [P, SLOTS, GT], I32)
        rel_bc = sb("rel_bc", [P, 2, GE], BF16)
        b_win = sb("b_win", [P, 2, H])
        base_sb = sb("base_sb", [1, G], I32)
        sweep_tab = sb("sweep_tab", [1, G, 2], I32)
        extra_sb = sb("extra_sb", [1, 4, G])
        flat = gath[:, :, :, :].rearrange("p a b c -> p (a b c)")
        dst_i, src_i = flat[:, 0:RE].bitcast(I32), flat[:, RE:2 * RE].bitcast(I32)
        rel_rows, src_f = flat[:, 2 * RE:3 * RE], flat[:, 3 * RE:4 * RE]
        rel_i, lo_i, hi_i = (flat[:, k * RE:k * RE + G * GT].bitcast(I32) for k in (0, 1, 3))
        LW = G * GT + 2 * DT
        hflat = hidden[:, :, :, :].rearrange("p a b c -> p (a b c)")
        lo_b, hi_b = hflat[:, 0:LW // 2].bitcast(BF16), hflat[:, LW // 2:LW].bitcast(BF16)
        deg = onehot_t[:, :, :].rearrange("p a b -> p (a b)")[0:U, 0:NP // U]
        deg_pool = flat[0:U, 2 * RE:2 * RE + NP // U]
        stats = onehot[:, :, :, :].rearrange("p a b c -> p (a b c)")[:, 0:NB * 6].rearrange(
            "p (b s) -> p b s", s=6)
        hot_flat = onehot[:, :, :, :].rearrange("p a b c -> p (a b c)")
        due, lead, least, none_far = (hot_flat[0:1, at:at + n] for at, n in (
            (1024, (ROUNDS + 2) * SLOTS), (1280, G), (1536, 1), (1544, 1)))
        a_rows = onehot_t[:, :, :].rearrange("p k (c f) -> p k c f", f=H)[:, :, 0:CB, :]
        b_rows = hidden[:, :, 0:CB, :]
        sweep_rel = hidden[:, 1, :, :].rearrange("p c f -> p (c f)")
        ident = sb("ident", [P, P])
        iota_w = sb("iota_w", [P, W])
        pidx = sb("pidx", [P, 1])
        lo_ref, hi_ref = sb("lo_ref", [P, U, DT], BF16), sb("hi_ref", [P, WU, DT], BF16)
        lo_hot, hi_hot = sb("lo_hot", [P, 2, U, DT], BF16), sb("hi_hot", [P, 2, WU, DT], BF16)
        far_w, far_u = sb("far_w", [P, FAR + 2]), sb("far_u", [P, FAR + 2])
        chunk_sums = sb("chunk_sums", [P, CN])
        ordered = sb("ordered", [1, 1], I32)
        select = sb("select", [U, WU, P])
        deg_stage = sb("deg_stage", [U, 2, HG * WU])
        far_col, far_hi = sb("far_col", [P, GT]), sb("far_hi", [P, GT], BF16)
        rel_rows_b = sb("rel_rows_b", [P, RE], BF16)
        gmin, gmax, base_f = (sb(n, [P, 2]) for n in ("gmin", "gmax", "base_f"))
        gmin_i, base_u, base_i, extra_i = (sb(n, [P, 2], I32) for n in ("gmin_i", "base_u", "base_i", "extra_i"))
        extra_f = sb("extra_f", [P, 2])
        cnt, root, dinv, rcnt, total, spread, var, std, rstd, shift = (sb(n, [P, NB]) for n in (
            "cnt", "root", "dinv", "rcnt", "total", "spread", "var", "std", "rstd", "shift"))
        w1_sb, w2_sb = sb("w1_sb", [D, D]), sb("w2_sb", [D, D])
        wab_sb, wself_sb = sb("wab_sb", [D, 2, H]), sb("wself_sb", [D, H])
        ew2_sb = sb("ew2_sb", [H, D])
        b1_bc, b2_bc, eb2_bc = sb("b1_bc", [P, D]), sb("b2_bc", [P, D]), sb("eb2_bc", [P, D])
        eb1_bc, eb1_col = sb("eb1_bc", [P, H]), sb("eb1_col", [P, 1])

        ps_e = ctx.enter_context(nc.psum_tensor("ps_e", [P, 2, 2 * 512], F32))
        ps_a = ctx.enter_context(nc.psum_tensor("ps_a", [P, 2, 512], F32))
        ps_z = ctx.enter_context(nc.psum_tensor("ps_z", [P, 2, 512], F32))

        dst_loaded, src_loaded, x_zeroed, weights_loaded = (sem(n) for n in (
            "dst_loaded", "src_loaded", "x_zeroed", "weights_loaded"))
        x_loaded = [sem(f"x_loaded_{k}") for k in range(len(X_PIECES))]
        consts_made, made_step, deg_zeroed = sem("consts_made"), sem("made_step"), sem("deg_zeroed")
        rel_ready, src_ready, rel_turned, src_turned, src_col_ready = (sem(n) for n in (
            "rel_ready", "src_ready", "rel_turned", "src_turned", "src_col_ready"))
        rel_b_ready, extra_ready = sem("rel_b_ready"), sem("extra_ready")
        base_stored, rel_stored, base_loaded, extra_loaded = (sem(n) for n in (
            "base_stored", "rel_stored", "base_loaded", "extra_loaded"))
        dve_step = sem("dve_step")
        sweep_tab_ready = sem("sweep_tab_ready")
        deg_hot_ready, deg_summed, deg_added, deg_turned, cnt_ready, root_ready = (sem(n) for n in (
            "deg_hot_ready", "deg_summed", "deg_added", "deg_turned", "cnt_ready", "root_ready"))
        var_ready, std_ready, shift_ready, x_normed = (sem(n) for n in (
            "var_ready", "std_ready", "shift_ready", "x_normed"))
        onehot_ready = {p: sem(f"onehot_ready_{p}") for p in PASSES[1:]}
        summed = {p: sem(f"summed_{p}") for p in PASSES[1:]}
        added = {p: sem(f"added_{p}") for p in PASSES[1:]}
        slot_ready = {p: sem(f"slot_ready_{p}") for p in PASSES[1:]}
        gathered = {p: [sem(f"gathered_{p}_{s}") for s in range(SLOTS)] for p in PASSES[1:]}
        gather_turn = sem("gather_turn")
        normalise_turn = sem("normalise_turn")
        root_turn = sem("root_turn")
        copy_turn = sem("copy_turn")
        transpose_turn = sem("transpose_turn")
        pass_done = {p: sem(f"pass_done_{p}") for p in PASSES}
        rows_ready = {p: sem(f"rows_ready_{p}") for p in PASSES[1:]}
        rows_turned = {p: sem(f"rows_turned_{p}") for p in PASSES[1:]}
        acc_started = {p: sem(f"acc_started_{p}") for p in PASSES[1:]}
        table_stored = {p: sem(f"table_stored_{p}") for p in CONVS}
        product_ready = {p: sem(f"product_ready_{p}") for p in PASSES[1:]}
        scaled = {p: sem(f"scaled_{p}") for p in CONVS}
        x_updated, x_biased = sem("x_updated"), sem("x_biased")
        deg_pool_zeroed, deg_staged = sem("deg_pool_zeroed"), sem("deg_staged")
        deg_added_pool, deg_summed_pool = sem("deg_added_pool"), sem("deg_summed_pool")
        wself_ready = sem("wself_ready")
        chunk_staged = {p: sem(f"chunk_staged_{p}") for p in PASSES[1:]}
        h_copied, self_ready = sem("h_copied"), sem("self_ready")
        a_ready, a_copied, b_ready, b_copied = (sem(n) for n in ("a_ready", "a_copied", "b_ready", "b_copied"))
        a_stored_early = sem("a_stored_early")
        a_stored = {when: [sem(f"a_stored_{when}_{k}") for k in range(2)] for when in ("unordered", "last")}
        stats_step = sem("stats_step")
        b_stored = [sem(f"b_stored_{k}") for k in range(2)]
        window_loaded = [sem(f"window_loaded_{k}") for k in range(2)]
        onehot_t_ready, expanded, messages_added, hidden_ready = (sem(n) for n in (
            "onehot_t_ready", "expanded", "messages_added", "hidden_ready"))
        out_ready, out_stored = sem("out_ready"), sem("out_stored")
        sw = {p: {n: sem(f"sweep_{n}_{p}") for n in (
            ("rel", "hot", "summed", "added") if p == "deg" else
            ("staged", "gathered", "rel", "hot", "summed", "added") if p in CONVS else
            ("staged", "gathered", "rel", "hot", "summed", "added",
             "loaded", "hot_t", "expanded", "messages", "hidden"))} for p in PASSES}

        def stored_chunks(sems, chunks):
            return [(sems[k], 16 * len([c for c in chunks if c % 2 == k])) for k in range(2)]

        def wait_first_rows(eng):
            flag = is_ordered(eng)
            with eng.If(flag > 0):
                eng.wait_ge(a_stored_early, 16 * AHEAD + 16)
            with eng.If(flag < 1):
                for what, value in stored_chunks(a_stored["unordered"], range(AHEAD)):
                    eng.wait_ge(what, value)

        def wait_source_table(eng):
            wait_first_rows(eng)
            for what, value in stored_chunks(a_stored["last"], range(AHEAD, CHUNKS)):
                eng.wait_ge(what, value)

        def late_lists(eng, body):
            with eng.If(is_ordered(eng) < 1):
                body(range(AHEAD), "unordered")
            body(range(AHEAD, CHUNKS), "last")

        def bcast(small, c, n=CB):
            return small[:, bass.ds(c, n)].unsqueeze(2).to_broadcast([P, n, D])

        def for_groups(eng, body, chunk=None):
            peeled = BEHIND * SLOTS if chunk else 0
            if chunk:
                flag = is_ordered(eng)
                with eng.Fori(0, peeled, SLOTS) as i:
                    for s in range(SLOTS):
                        body(i + s, s)
            with eng.Fori(peeled, MAIN, SLOTS) as i:
                for s in range(SLOTS):
                    body(i + s, s)
                    if chunk and s in chunk:
                        with eng.If(flag > 0):
                            chunk[s]((i - peeled) // SLOTS, i)
            for g in range(MAIN, G):
                body(g, g % SLOTS)
                if chunk and g % SLOTS in chunk and g // SLOTS < AHEAD + BEHIND:
                    with eng.If(flag > 0):
                        chunk[g % SLOTS](g // SLOTS - BEHIND, g // SLOTS * SLOTS)

        def is_ordered(eng):
            eng.wait_ge(sweep_tab_ready, 1)
            return eng.value_load(ordered[0:1, 0:1], min_val=0, max_val=1)

        def late_chunks(eng, body, chunks=CHUNKS):
            with eng.If(is_ordered(eng) < 1):
                for c in range(AHEAD):
                    body(c, c % 2)
            for c in range(AHEAD, chunks):
                body(c, c % 2)

        def for_chunks(eng, body):
            with eng.Fori(0, CHUNKS - 1, 2) as i:
                for k in range(2):
                    body(i + k, k)
            body(CHUNKS - 1, 0)

        def sweep(eng, body):
            eng.wait_ge(sweep_tab_ready, 1)
            many = eng.value_load(sweep_tab[0:1, G - 1, 1:2], min_val=0, max_val=G * FAR)
            with eng.If(many > 0):
                with eng.Fori(0, G) as g:
                    first = eng.value_load(sweep_tab[0:1, bass.ds(g, 1), 0:1].rearrange("p a b -> p (a b)"),
                                           min_val=0, max_val=G * FAR)
                    end = eng.value_load(sweep_tab[0:1, bass.ds(g, 1), 1:2].rearrange("p a b -> p (a b)"),
                                         min_val=0, max_val=G * FAR)
                    with eng.If(first < end):
                        with eng.Fori(first, end) as n:
                            body(g, n, within(n - first + 1, 1, FAR))

        def within(value, low, high):
            return nc.s_assert_within(value, low, high, skip_runtime_bounds_check_because=
                                      "the table holds windows up to the group's greatest target")

        def load_base(eng, g):
            return nc.s_assert_within(eng.value_load(base_sb[0:1, bass.ds(g, 1)]), 0, BASE_MAX,
                                      skip_runtime_bounds_check_because="targets are nodes, at most N - 1")

        def far_base(eng, g, j):
            return within(load_base(eng, g) + j * WU, 0, BASE_MAX)

        block = ctx.enter_context(nc.Block())

        @block.sync
        def _(sp):
            def load_edges(staged, edges, loaded):
                lead = FULL // 16 * 16
                sp.dma_start(staged[0:lead, :], edges[0:lead * RE].rearrange("(p e) -> p e", e=RE)
                             ).then_inc(loaded, 16)
                if lead < FULL:
                    sp.dma_start(staged[lead:FULL, :], edges[lead * RE:FULL * RE].rearrange("(p e) -> p e", e=RE)
                                 ).then_inc(loaded, 16)
                at, start, n = 0, FULL * RE, LEFT
                while at < RE:
                    sp.dma_start(staged[FULL:R, at:at + n], edges[start:start + n].rearrange("(p e) -> p e", p=1)
                                 ).then_inc(loaded, 16)
                    at, start, n = at + n, E - LASTG, min(LASTG, RE - at - n)

            load_edges(dst_i, dst, dst_loaded)
            for k, (first, end) in enumerate(X_PIECES):
                full = min(end, N // P)
                sp.dma_start(x_sb[:, first:full, :], x[first * P:full * P, :].rearrange("(b p) d -> p b d", p=P)
                             ).then_inc(x_loaded[k], 16)
            sp.wait_ge(x_zeroed, 1)
            sp.dma_start(x_sb[0:N % P, N // P, :], x[N // P * P:N, :]).then_inc(x_loaded[-1], 16)
            load_edges(src_i, src, src_loaded)
            sp.wait_ge(rel_ready, 1)
            sp.dma_start(base_row.rearrange("(r k) -> r k", k=2), base_u[0:R, :]).then_inc(base_stored, 16)
            sp.wait_ge(base_stored, 16)
            sp.dma_start(base_sb[:, :], base_row.rearrange("(a g) -> a g", a=1)).then_inc(base_loaded, 16)
            sp.dma_start(rel_row_f.rearrange("(r k) e -> r (k e)", k=2), rel_rows[0:R, :]).then_inc(rel_stored, 16)
            sp.wait_ge(extra_ready, 1)
            sp.dma_start(extra_row.rearrange("(r k) -> r k", k=2), extra_f[0:R, :]).then_inc(base_stored, 16)
            sp.wait_ge(base_stored, 32)
            sp.dma_start(extra_sb[0:1, 0, :], extra_row.rearrange("(a g) -> a g", a=1)).then_inc(extra_loaded, 16)
            sp.wait_ge(rel_b_ready, 1)
            sp.dma_start(rel_row_b.rearrange("(r k) e -> r (k e)", k=2), rel_rows_b[0:R, :]).then_inc(rel_stored, 16)

            for c in range(0, CHUNKS, TABLE_PIECE):
                sp.wait_ge(rows_ready["conv1"], c + TABLE_PIECE)
                sp.dma_start(u_tab["conv1"][c * CN:(c + TABLE_PIECE) * CN, :].rearrange("(b p) d -> p b d", p=P),
                             t_sb[:, c * CB:(c + TABLE_PIECE) * CB, :]).then_inc(table_stored["conv1"], 16)

            def store_table(c, k):
                sp.wait_ge(rows_ready["conv2"], c + 1)
                sp.dma_start(u_tab["conv2"][bass.ds(c * CN, CN), :].rearrange("(b p) d -> p b d", p=P),
                             t_sb[:, bass.ds(c * CB, CB), :]).then_inc(table_stored["conv2"], 16)
            for_chunks(sp, store_table)

            def store_chunk(table, rows, copied, stored):
                def body(c, k):
                    sp.wait_ge(copied, c + 3)
                    sp.dma_start(table[bass.ds(c * CN, CN), :].rearrange("(b p) f -> p b f", p=P),
                                 rows[:, k]).then_inc(stored[k], 16)
                for_chunks(sp, body)
            def store_source(c, k, stored):
                sp.wait_ge(a_copied, c + 3)
                sp.dma_start(a_tab[bass.ds(c * CN, CN), :].rearrange("(b p) f -> p b f", p=P),
                             a_rows[:, k]).then_inc(stored, 16)

            def store_sources(chunks, when):
                for c in chunks:
                    store_source(c, c % 2, a_stored[when][c % 2])
            with sp.If(is_ordered(sp) > 0):
                with sp.Fori(0, AHEAD) as c:
                    store_source(c, 0, a_stored_early)
            late_lists(sp, store_sources)
            store_chunk(b_tab, b_rows, b_copied, b_stored)
            for what, value in stored_chunks(b_stored, range(CHUNKS)) + [(rel_stored, 32)]:
                sp.wait_ge(what, value)

            def load_window(g, s):
                k = s % 2
                sp.wait_ge(expanded, g + 1)
                sp.dma_start(b_win[:, k, :], b_tab[bass.ds(load_base(sp, g) * U, W), :]
                             ).then_inc(window_loaded[k], 16)
                sp.dma_start(rel_bc[:, k, :], rel_row_b[bass.ds(g, 1), :].to_broadcast([P, GE])
                             ).then_inc(window_loaded[k], 16)
            def store_out(c, k=0):
                sp.wait_ge(out_ready, c + 2)
                sp.dma_start(out[bass.ds(c * CN, CN), :].rearrange("(b p) d -> p b d", p=P),
                             t_sb[:, bass.ds(c * CB, CB), :]).then_inc(out_stored, 16)
            for_groups(sp, load_window, {SLOTS - 1: lambda c, g: store_out(c)})

            def sweep_load(g, n, j):
                sp.wait_ge(sw["edge"]["added"], n + 1)
                sp.dma_start(b_win[:, 0, :], b_tab[bass.ds(far_base(sp, g, j) * U, W), :]
                             ).then_inc(sw["edge"]["loaded"], 16)
                sp.dma_start(sweep_rel, rel_row_f[bass.ds(g, 1), :].to_broadcast([P, GE])
                             ).then_inc(sw["edge"]["loaded"], 16)
            sweep(sp, sweep_load)

            late_chunks(sp, store_out, N // CN)
            sp.wait_ge(out_ready, CHUNKS + 1)
            last_blocks = range(N // CN * CB, -(-N // P))
            for b in last_blocks:
                rows = min(P, N - b * P)
                sp.dma_start(out[b * P:b * P + rows, :], t_sb[0:rows, b, :]).then_inc(out_stored, 16)
            sp.wait_ge(out_stored, 16 * (N // CN + len(last_blocks)))

        @block.gpsimd
        def _(pool):
            exact = dict(allow_small_or_imprecise_dtypes=True)
            pool.memset(ident[:, :], 0.0).then_inc(made_step, 1)
            pool.memset(select[:, :, :], 0.0).then_inc(made_step, 1)
            pool.memset(x_sb[:, N // P:NB, :], 0.0).then_inc(x_zeroed, 1)
            pool.wait_ge(made_step, 2)
            pool.affine_select(out=ident[:, :], in_=ident[:, :], compare_op=ALU.not_equal, fill=1.0,
                               base=0, pattern=[[-1, P]], channel_multiplier=1).then_inc(consts_made, 1)
            pool.iota(lo_ref[:, :, :], pattern=[[1, U], [0, DT]], base=0, channel_multiplier=0,
                      **exact).then_inc(consts_made, 1)
            pool.iota(hi_ref[:, :, :], pattern=[[1, WU], [0, DT]], base=0, channel_multiplier=0,
                      **exact).then_inc(consts_made, 1)
            pool.memset(deg, 0.0).then_inc(deg_zeroed, 1)
            pool.iota(iota_w[:, :], pattern=[[1, W]], base=0, channel_multiplier=0, **exact).then_inc(consts_made, 1)
            pool.iota(pidx[:, :], pattern=[[1, 1]], base=0, channel_multiplier=1, **exact).then_inc(consts_made, 1)
            pool.iota(far_w[:, :], pattern=[[W, FAR + 2]], base=0, channel_multiplier=0,
                      **exact).then_inc(consts_made, 1)
            pool.iota(far_u[:, :], pattern=[[WU, FAR + 2]], base=0, channel_multiplier=0,
                      **exact).then_inc(consts_made, 1)
            pool.iota(due, pattern=[[CN // U, ROUNDS + 2], [0, SLOTS]], base=(1 - BEHIND) * CN // U,
                      channel_multiplier=0, **exact).then_inc(consts_made, 1)
            pool.affine_select(out=select[:, :, :], in_=select[:, :, :], compare_op=ALU.not_equal, fill=1.0,
                               base=0, pattern=[[U, WU], [-1, P]], channel_multiplier=1).then_inc(consts_made, 1)

            def gather_group(table, width, s, n, done):
                for c in range(n):
                    pool.indirect_dma_start(
                        out=gath[:, s, c, 0:width], out_offset=None, in_=table,
                        in_offset=bass.IndirectOffsetOnAxis(ap=idx[:, s, c:c + 1], axis=0)).then_inc(done, 16)

            def gather_pass(p, table, width):
                def body(g, s):
                    pool.wait_ge(slot_ready[p], g + 1)
                    pool.sem_inc(gather_turn, 1)
                    gather_group(table, width, s, tiles(g), gathered[p][s])
                for_groups(pool, body)

                def sweep_gather(g, n, j):
                    pool.wait_ge(sw[p]["staged"], n + 1)
                    pool.sem_inc(gather_turn, 1)
                    gather_group(table, width, 0, GT, sw[p]["gathered"])
                sweep(pool, sweep_gather)

            pool.wait_ge(rel_turned, 1)
            pool.wait_ge(rel_stored, 32)
            pool.memset(deg_pool, 0.0).then_inc(deg_pool_zeroed, 1)
            pool.wait_ge(deg_pool_zeroed, 1)
            pool.wait_ge(base_loaded, 16)
            pool.sem_inc(deg_added_pool, HG + 1)

            def deg_step(q, k):
                pool.wait_ge(deg_staged, q + 3)
                for j in range(HG):
                    pool.wait_ge(deg_added_pool, q * HG + j + HG + 1)
                    window = deg_pool[:, bass.ds(load_base(pool, q * DG + HG + j), WU)]
                    pool.tensor_tensor(window, deg_stage[:, k, j * WU:(j + 1) * WU], window, ALU.add
                                       ).then_inc(deg_added_pool, 1)
            with pool.Fori(0, DSTEPS - 1, 2) as i:
                for k in range(2):
                    deg_step(i + k, k)
            deg_step(DSTEPS - 1, 0)

            for p in CONVS:
                pool.wait_ge(table_stored[p], 16 * STORES[p])
                gather_pass(p, u_tab[p], D)
            wait_source_table(pool)
            gather_pass("edge", a_tab, H)

        @block.vector
        def _(dve):
            steps = [0]

            def link(ins):
                steps[0] += 1
                ins.then_inc(dve_step, 1)
                dve.wait_ge(dve_step, steps[0])

            def halves(ap):
                return [ap[0:R, k * GE:(k + 1) * GE] for k in range(2)]

            dve.wait_ge(dst_loaded, 16 * EDGE_LOADS)
            link(dve.tensor_reduce(gmin[0:R, :], dst_i[0:R, :].rearrange("p (k e) -> p k e", k=2), AX_X, ALU.min))
            link(dve.tensor_copy(gmin_i[0:R, :], gmin[0:R, :]))
            link(dve.tensor_scalar(base_u[0:R, :], gmin_i[0:R, :], 3, None, ALU.arith_shift_right))
            link(dve.tensor_scalar(base_i[0:R, :], base_u[0:R, :], 3, None, ALU.logical_shift_left))
            link(dve.tensor_copy(base_f[0:R, :], base_i[0:R, :]))
            for k in range(2):
                last = dve.tensor_scalar(halves(rel_rows)[k], halves(dst_i)[k], base_f[0:R, k:k + 1], None,
                                         ALU.subtract)
            last.then_inc(rel_ready, 1)
            link(dve.tensor_reduce(gmax[0:R, :], dst_i[0:R, :].rearrange("p (k e) -> p k e", k=2), AX_X, ALU.max))
            link(dve.tensor_tensor(gmax[0:R, :], gmax[0:R, :], base_f[0:R, :], ALU.subtract))
            link(dve.tensor_copy(extra_i[0:R, :], gmax[0:R, :]))
            link(dve.tensor_scalar(extra_i[0:R, :], extra_i[0:R, :], 7, None, ALU.arith_shift_right))
            dve.tensor_copy(extra_f[0:R, :], extra_i[0:R, :]).then_inc(extra_ready, 1)
            dve.tensor_copy(rel_rows_b[0:R, :], rel_rows[0:R, :]).then_inc(rel_b_ready, 1)

            def row_stats(b):
                return dve.bn_stats(stats[:, b, :], x_sb[:, b, :])

            def take_variance(s, follow):
                dve.tensor_tensor(total[:, s], stats[:, s, 1], stats[:, s, 4], ALU.add)
                dve.tensor_tensor(spread[:, s], stats[:, s, 1], stats[:, s, 4], ALU.subtract)
                follow(dve.tensor_tensor(var[:, s], stats[:, s, 2], stats[:, s, 5], ALU.add))
                dve.tensor_tensor(spread[:, s], spread[:, s], spread[:, s], ALU.mult)
                follow(dve.tensor_scalar(var[:, s], var[:, s], 1.0 / D, EPS, ALU.mult, ALU.add))
                return dve.scalar_tensor_tensor(out=var[:, s], in0=spread[:, s], scalar=0.25, in1=var[:, s],
                                                op0=ALU.mult, op1=ALU.add)

            def take_shift(s, follow):
                follow(dve.reciprocal(rstd[:, s], std[:, s]))
                return dve.scalar_tensor_tensor(out=shift[:, s], in0=total[:, s], scalar=-0.5, in1=rstd[:, s],
                                                op0=ALU.mult, op1=ALU.mult)

            dve.wait_ge(rel_turned, 1)
            for j in range(4):
                last = dve.tensor_copy(
                    rel_col[:, :].rearrange("p (r kc) -> p kc r", kc=2 * GT)[:, 4 * j:4 * j + 4, :],
                    ps_e[:, j // 2, (j % 2) * 512:(j % 2) * 512 + 4 * R].rearrange("p (a r) -> p a r", a=4))
            link(last)
            full, part = E // P, E % P
            link(dve.memset(rel_col[part:P, full:full + 1], -1.0))
            link(dve.memset(rel_col[:, full + 1:G * GT], -1.0))
            for k, (first, end) in enumerate(X_PIECES):
                dve.wait_ge(x_loaded[k], 32 if end == NB else 16)
                for b in range(first, end):
                    last = row_stats(b)
            link(last)
            take_variance(slice(0, NB), link).then_inc(var_ready, 1)
            link(dve.tensor_copy(rel_i, rel_col[:, :]))
            dve.wait_ge(src_turned, 1)
            dve.tensor_scalar(lo_i, rel_i, U - 1, None, ALU.bitwise_and)
            link(dve.tensor_scalar(hi_i, rel_i, 3, None, ALU.arith_shift_right))
            dve.tensor_copy(lo_b[:, 0:G * GT], lo_i)
            link(dve.tensor_copy(hi_b[:, 0:G * GT], hi_i))

            def deg_hot(q, k):
                dve.tensor_tensor(lo_hot[:, k], lo_ref[:, :, :],
                                  lo_b[:, bass.ds(q * DT, DT)].unsqueeze(1).to_broadcast([P, U, DT]), ALU.is_equal)
                dve.tensor_tensor(hi_hot[:, k], hi_ref[:, :, :],
                                  hi_b[:, bass.ds(q * DT, DT)].unsqueeze(1).to_broadcast([P, WU, DT]),
                                  ALU.is_equal).then_inc(deg_hot_ready, 1)

            def deg_step(q, k):
                if not (isinstance(q, int) and q + 1 >= DSTEPS):
                    dve.wait_ge(deg_staged, q + 2)
                    deg_hot(q + 1, (k + 1) % 2)
                dve.wait_ge(deg_summed, q + 1)
                for j in range(HG):
                    dve.wait_ge(deg_added, q * HG + j + HG + 1)
                    window = deg[:, bass.ds(load_base(dve, q * DG + j), WU)]
                    dve.tensor_tensor(window, ps_a[0:U, k, j * WU:(j + 1) * WU], window, ALU.add
                                      ).then_inc(deg_added, 1)

            dve.wait_ge(consts_made, 9)
            dve.wait_ge(deg_zeroed, 1)
            dve.wait_ge(base_loaded, 16)
            dve.sem_inc(deg_added, HG + 1)
            deg_hot(0, 0)
            dve.wait_ge(std_ready, 1)
            take_shift(slice(0, NB), link).then_inc(shift_ready, 1)
            dve.wait_ge(extra_loaded, 16)
            link(dve.memset(extra_sb[0:1, 1, :], 0.0))
            link(dve.tensor_tensor_scan(extra_sb[0:1, 2, :], extra_sb[0:1, 0, :], extra_sb[0:1, 1, :], 0.0,
                                        ALU.add, ALU.add))
            link(dve.tensor_tensor(extra_sb[0:1, 3, :], extra_sb[0:1, 2, :], extra_sb[0:1, 0, :], ALU.subtract))
            link(dve.tensor_copy(sweep_tab[0:1, :, 1], extra_sb[0:1, 2, :]))
            link(dve.tensor_copy(sweep_tab[0:1, :, 0], extra_sb[0:1, 3, :]))
            link(dve.tensor_copy(lead, base_sb[0:1, :]))
            link(dve.tensor_tensor(lead, lead, due[:, 0:G], ALU.subtract))
            link(dve.tensor_reduce(least, lead, AX_X, ALU.min))
            link(dve.tensor_scalar(least, least, 0.0, None, ALU.is_ge))
            link(dve.tensor_scalar(none_far, extra_sb[0:1, 2, G - 1:G], 0.0, None, ALU.is_equal))
            dve.tensor_tensor(ordered[:, :], least, none_far, ALU.mult).then_inc(sweep_tab_ready, 1)
            with dve.Fori(0, DSTEPS - 1, 2) as i:
                for k in range(2):
                    deg_step(i + k, k)
            deg_step(DSTEPS - 1, 0)
            dve.wait_ge(deg_added, DSTEPS * HG + HG + 1)
            dve.wait_ge(deg_added_pool, DSTEPS * HG + HG + 1)
            link(dve.tensor_tensor(deg, deg, deg_pool, ALU.add))
            def sweep_deg(g, n, j):
                s = sw["deg"]
                dve.tensor_copy(far_col[:, :], hi_i[:, bass.ds(g * GT, GT)]).then_inc(s["rel"], 1)
                dve.wait_ge(s["rel"], n * 2 + 1)
                dve.tensor_scalar(far_hi[:, :], far_col[:, :], far_u[:, bass.ds(j, 1)], None, ALU.subtract
                                  ).then_inc(s["rel"], 1)
                dve.wait_ge(s["rel"], n * 2 + 2)
                dve.tensor_tensor(lo_hot[:, 0, :, 0:GT], lo_ref[:, :, 0:GT],
                                  lo_b[:, bass.ds(g * GT, GT)].unsqueeze(1).to_broadcast([P, U, GT]), ALU.is_equal)
                dve.tensor_tensor(hi_hot[:, 0, :, 0:GT], hi_ref[:, :, 0:GT],
                                  far_hi[:, :].unsqueeze(1).to_broadcast([P, WU, GT]), ALU.is_equal
                                  ).then_inc(s["hot"], 1)
                dve.wait_ge(s["summed"], n + 1)
                window = deg[:, bass.ds(far_base(dve, g, j), WU)]
                dve.tensor_tensor(window, ps_a[0:U, 0, 0:WU], window, ALU.add).then_inc(s["added"], 1)
                dve.wait_ge(s["added"], n + 1)
            sweep(dve, sweep_deg)
            dve.sem_inc(pass_done["deg"], 1)

            dve.wait_ge(deg_turned, 1)
            dve.tensor_scalar(cnt[:, :], ps_z[:, 0, 0:NB], 1.0, None, ALU.add).then_inc(cnt_ready, 1)
            dve.wait_ge(root_ready, 1)
            link(dve.reciprocal(dinv[:, :], root[:, :]))
            dve.wait_ge(x_normed, DSTEPS + 1)
            for c in range(0, CHUNKS, TABLE_PIECE):
                rows = t_sb[:, c * CB:(c + TABLE_PIECE) * CB, :]
                dve.tensor_tensor(rows, rows, bcast(dinv, c * CB, TABLE_PIECE * CB), ALU.mult
                                  ).then_inc(rows_ready["conv1"], TABLE_PIECE)
            dve.reciprocal(rcnt[:, :], cnt[:, :])

            def make_onehot(p, g, k):
                n = tiles(g)
                dve.tensor_tensor(onehot[:, k, 0:n, :], iota_w[:, :].unsqueeze(1).to_broadcast([P, n, W]),
                                  rel_col[:, bass.ds(g * GT, n)].unsqueeze(2).to_broadcast([P, n, W]),
                                  ALU.is_equal).then_inc(onehot_ready[p], 1)

            def add_window(p, g, k, rows):
                dve.wait_ge(summed[p], g + 1)
                dve.wait_ge(added[p], g + 2)
                window = acc[0:rows, bass.ds(load_base(dve, g) * U, W)]
                dve.tensor_tensor(window, ps_a[0:rows, k, 0:W], window, ALU.add).then_inc(added[p], 1)

            def stage(p, g, s):
                dve.tensor_copy(idx[:, s, :], src_col[:, bass.ds(g * GT, GT)]).then_inc(slot_ready[p], 1)

            def stage_next(p, g, s):
                if not isinstance(g, int) or g + SLOTS < G:
                    stage(p, g + SLOTS, s)

            def sweep_sums(p, rows, messages=None):
                s = sw[p]
                dve.wait_ge(added[p], G + 2)
                dve.sem_inc(s["added"], 1)

                def body(g, n, j):
                    dve.tensor_copy(idx[:, 0, :], src_col[:, bass.ds(g * GT, GT)]).then_inc(s["staged"], 1)
                    dve.tensor_scalar(far_col[:, :], rel_col[:, bass.ds(g * GT, GT)], far_w[:, bass.ds(j, 1)],
                                      None, ALU.subtract).then_inc(s["rel"], 1)
                    dve.wait_ge(s["rel"], n + 1)
                    dve.tensor_tensor(onehot[:, 0], iota_w[:, :].unsqueeze(1).to_broadcast([P, GT, W]),
                                      far_col[:, :].unsqueeze(2).to_broadcast([P, GT, W]), ALU.is_equal
                                      ).then_inc(s["hot"], 1)
                    if messages:
                        messages(g, n, j)
                    dve.wait_ge(s["summed"], n + 1)
                    window = acc[0:rows, bass.ds(far_base(dve, g, j) * U, W)]
                    dve.tensor_tensor(window, ps_a[0:rows, 0, 0:W], window, ALU.add).then_inc(s["added"], 1)
                    dve.wait_ge(s["added"], n + 2)
                sweep(dve, body)
                dve.sem_inc(pass_done[p], 1)

            def conv_sums(p, chunk=None):
                for s in range(SLOTS):
                    stage(p, s, s)
                make_onehot(p, 0, 0)
                dve.wait_ge(acc_started[p], 2 + CHUNKS)
                dve.sem_inc(added[p], 2)

                def body(g, s):
                    if not (isinstance(g, int) and g + 1 >= G):
                        make_onehot(p, g + 1, (s + 1) % 2)
                    add_window(p, g, s % 2, D)
                    stage_next(p, g, s)
                for_groups(dve, body, chunk)
                sweep_sums(p, D)

            def scale_rows(p, c, k, factor, other):
                dve.wait_ge(product_ready[p], c + 1)
                for j in range(CB):
                    b = bass.ds(c * CB + j, 1)
                    last = dve.scalar_tensor_tensor(
                        out=t_sb[:, b, :].rearrange("p a d -> p (a d)"), in0=ps_z[:, k, j * D:(j + 1) * D],
                        scalar=factor[:, b], in1=other(b), op0=ALU.mult, op1=ALU.add)
                last.then_inc(scaled[p], 1)
                return t_sb[:, bass.ds(c * CB, CB), :]

            def second_table(c, k):
                rows = scale_rows("conv1", c, k, dinv, lambda b: b1_bc[:, :])
                dve.wait_ge(scaled["conv1"], c + 3)
                dve.scalar_tensor_tensor(out=rows, in0=rows, scalar=0.0, in1=bcast(dinv, c * CB),
                                         op0=ALU.max, op1=ALU.mult).then_inc(rows_ready["conv2"], 1)

            dve.wait_ge(src_col_ready, 1)
            dve.wait_ge(weights_loaded, 16 * 9)
            dve.wait_ge(table_stored["conv1"], 16 * STORES["conv1"])
            dve.sem_inc(scaled["conv1"], 2)
            conv_sums("conv1", {3: lambda c, g: second_table(c, 0)})
            late_chunks(dve, second_table)
            STEPS = 4

            def follower(c, n, first):
                step = [first]

                def follow(ins):
                    step[0] += 1
                    ins.then_inc(stats_step, n)
                    dve.wait_ge(stats_step, c * STEPS + step[0] * n)
                return follow

            def update_x(c, k):
                rows = scale_rows("conv2", c, k, dinv, lambda b: b2_bc[:, :])
                dve.wait_ge(scaled["conv2"], c + 3)
                xs = x_sb[:, bass.ds(c * CB, CB), :]
                dve.scalar_tensor_tensor(out=xs, in0=rows, scalar=0.0, in1=xs, op0=ALU.max, op1=ALU.add
                                         ).then_inc(x_updated, 1)
                dve.wait_ge(x_updated, c + 1)
                for j in range(CB):
                    b = bass.ds(c * CB + j, 1)
                    last = dve.bn_stats(stats[:, b, :].rearrange("p a s -> p (a s)"),
                                        x_sb[:, b, :].rearrange("p a d -> p (a d)"))
                return last

            def finish_variance(last, c, n):
                follow = follower(c, n, 0)
                follow(last)
                take_variance(bass.ds(c * CB, n * CB), follow).then_inc(var_ready, n)

            def finish_shift(c, n):
                dve.wait_ge(std_ready, c + n + 1)
                take_shift(bass.ds(c * CB, n * CB), follower(c, n, STEPS - 1)).then_inc(shift_ready, n)

            def update_list(chunks, when):
                for c in chunks:
                    last = update_x(c, c % 2)
                finish_variance(last, chunks[0], len(chunks))
                finish_shift(chunks[0], len(chunks))

            dve.wait_ge(table_stored["conv2"], 16 * CHUNKS)
            dve.sem_inc(scaled["conv2"], 2)
            conv_sums("conv2", {2: lambda c, g: finish_variance(update_x(c, 0), c, 1),
                                3: lambda c, g: finish_shift(c, 1)})
            late_lists(dve, update_list)
            dve.tensor_tensor(wself_sb[:, :], wab_sb[:, 0, :], wab_sb[:, 1, :], ALU.add).then_inc(wself_ready, 1)
            for s in range(SLOTS):
                stage("edge", s, s)
            make_onehot("edge", 0, 0)
            make_onehot("edge", 1, 1)
            dve.sem_inc(b_copied, 2)
            for c in range(CHUNKS):
                k = c % 2
                dve.wait_ge(b_ready, c + 1)
                if c >= 2:
                    dve.wait_ge(b_stored[k], 16 * (c // 2))
                dve.tensor_tensor(b_rows[:, k], ps_z[:, k, :].rearrange("p (b f) -> p b f", f=H),
                                  eb1_bc[:, :].unsqueeze(1).to_broadcast([P, CB, H]), ALU.add
                                  ).then_inc(b_copied, 1)

            def make_onehot_t(g, s):
                k = s % 2
                dve.wait_ge(window_loaded[k], (uses(g, s, 2) + 1) * 32)
                dve.tensor_scalar(onehot_t[:, k, :], rel_bc[:, k, :], pidx[:, 0:1], None,
                                  ALU.is_equal).then_inc(onehot_t_ready, 1)

            def gathered_count(g, s):
                if isinstance(g, int):
                    return 16 * (GT * (g // SLOTS) + tiles(g))
                return uses(g, s, SLOTS) * (16 * GT) + 16 * GT

            def add_messages(g, s):
                k, n = s % 2, tiles(g)
                dve.wait_ge(expanded, g + 3)
                dve.wait_ge(gathered["edge"][s], gathered_count(g, s))
                dve.tensor_tensor(hidden[:, k, 0:n, :], ps_e[:, k, 0:n * H].rearrange("p (c f) -> p c f", f=H),
                                  gath[:, s, 0:n, :], ALU.add).then_inc(messages_added, 1)
                stage_next("edge", g, s)

            wait_source_table(dve)
            for what, value in stored_chunks(b_stored, range(CHUNKS)):
                dve.wait_ge(what, value)
            dve.sem_inc(messages_added, 1)
            for g in range(2):
                make_onehot_t(g, g)
            for g in range(2):
                add_messages(g, g)
            dve.wait_ge(rows_ready["edge"], CHUNKS)
            dve.tensor_tensor(x_sb[:, :, :], x_sb[:, :, :],
                              eb2_bc[:, :].unsqueeze(1).to_broadcast([P, NB, D]), ALU.add).then_inc(x_biased, 1)
            dve.wait_ge(acc_started["edge"], 2 + CHUNKS)
            dve.sem_inc(added["edge"], 2)

            def edge_group(g, s):
                two_ahead = not isinstance(g, int) or g + 2 < G
                if two_ahead:
                    make_onehot_t(g + 2, (s + 2) % SLOTS)
                add_window("edge", g, s % 2, H)
                if two_ahead:
                    make_onehot("edge", g + 2, s % 2)
                    add_messages(g + 2, (s + 2) % SLOTS)
            def finish(c, k):
                dve.wait_ge(product_ready["edge"], c + 1)
                for j in range(CB):
                    b = bass.ds(c * CB + j, 1)
                    last = dve.scalar_tensor_tensor(
                        out=t_sb[:, b, :].rearrange("p a d -> p (a d)"), in0=ps_z[:, k, j * D:(j + 1) * D],
                        scalar=rcnt[:, b], in1=x_sb[:, b, :].rearrange("p a d -> p (a d)"),
                        op0=ALU.mult, op1=ALU.add)
                last.then_inc(out_ready, 1)

            dve.wait_ge(x_biased, 1)
            dve.sem_inc(out_ready, 1)
            for_groups(dve, edge_group, {3: lambda c, g: finish(c, 0)})

            def sweep_messages(g, n, j):
                s = sw["edge"]
                dve.wait_ge(s["loaded"], n * 32 + 32)
                dve.tensor_scalar(onehot_t[:, 0, :], sweep_rel, far_w[:, bass.ds(j, 1)], pidx[:, 0:1],
                                  ALU.subtract, ALU.is_equal).then_inc(s["hot_t"], 1)
                dve.wait_ge(s["expanded"], n + 1)
                dve.wait_ge(s["gathered"], n * (16 * GT) + 16 * GT)
                dve.tensor_tensor(hidden[:, 0], ps_e[:, 0, :].rearrange("p (c f) -> p c f", f=H),
                                  gath[:, 0], ALU.add).then_inc(s["messages"], 1)
            sweep_sums("edge", H, sweep_messages)

            late_chunks(dve, finish)

        @block.scalar
        def _(act):
            for t, d in ((w1_sb[:, :], w1), (w2_sb[:, :], w2), (ew2_sb[:, :], ew2),
                         (wab_sb[:, :, :], ew1.rearrange("(k d) f -> d k f", k=2)),
                         (b1_bc[:, :], b1.partition_broadcast(P)), (b2_bc[:, :], b2.partition_broadcast(P)),
                         (eb2_bc[:, :], eb2.partition_broadcast(P)), (eb1_bc[:, :], eb1.partition_broadcast(P)),
                         (eb1_col[:, :], eb1.rearrange("(p a) -> p a", a=1))):
                act.dma_start(t, d).then_inc(weights_loaded, 16)
            act.wait_ge(src_loaded, 16 * EDGE_LOADS)
            act.activation(src_f[0:R, :], src_i[0:R, :], ACT.Copy).then_inc(src_ready, 1)
            act.wait_ge(src_turned, 1)
            for j in range(4):
                ps = (ps_a, ps_z)[j // 2]
                last = act.activation(
                    src_col[:, 0:G * GT].rearrange("p (r kc) -> p kc r", kc=2 * GT)[:, 4 * j:4 * j + 4, :],
                    ps[:, j % 2, 0:4 * R].rearrange("p (a r) -> p a r", a=4), ACT.Copy)
            last.then_inc(src_col_ready, 1)

            def take_root(s, turn, n=1):
                act.wait_ge(var_ready, turn)
                act.sem_inc(root_turn, 1)
                act.activation(std[:, s], var[:, s], ACT.Sqrt).then_inc(std_ready, n)

            def normalise(b, rows=None):
                b = bass.ds(b, 1)
                return act.activation(t_sb[:, b, :].rearrange("p a d -> p (a d)") if rows is None else rows,
                                      x_sb[:, b, :].rearrange("p a d -> p (a d)"), ACT.Relu,
                                      scale=rstd[:, b], bias=shift[:, b])

            take_root(slice(0, NB), 1)
            act.wait_ge(shift_ready, 1)
            act.sem_inc(deg_staged, 2)

            def deg_step(q, k):
                for j in range(2):
                    last = normalise(q * 2 + j)
                last.then_inc(x_normed, 1)
                act.wait_ge(deg_summed_pool, q + 1)
                act.wait_ge(deg_added_pool, q * HG + 1)
                act.activation(deg_stage[:, k, :], ps_z[0:U, k, 0:HG * WU], ACT.Copy).then_inc(deg_staged, 1)
            with act.Fori(0, DSTEPS - 1, 2) as i:
                for k in range(2):
                    deg_step(i + k, k)
            deg_step(DSTEPS - 1, 0)
            for b in range(2 * DSTEPS, NB):
                last = normalise(b)
            last.then_inc(x_normed, 1)
            act.wait_ge(cnt_ready, 1)
            act.activation(root[:, :], cnt[:, :], ACT.Sqrt).then_inc(root_ready, 1)

            def stage_chunk(p, c, rows, g):
                act.wait_ge(added[p], g + 2)
                act.activation(chunk_sums[0:rows, :], acc[0:rows, bass.ds(c * CN, CN)], ACT.Copy
                               ).then_inc(chunk_staged[p], 1)

            def start_from_own(p):
                act.sem_inc(acc_started[p], 2)

                def start_acc(c, k):
                    act.wait_ge(rows_turned[p], c + 1)
                    act.activation(acc[0:D, bass.ds(c * CN, CN)], ps_e[0:D, k, 0:CN], ACT.Copy
                                   ).then_inc(acc_started[p], 1)
                for_chunks(act, start_acc)

            start_from_own("conv1")
            with act.If(is_ordered(act) > 0):
                with act.Fori(0, AHEAD) as c:
                    act.wait_ge(scaled["conv1"], c + 2)
                    stage_chunk("conv1", c, D, c * SLOTS + BEHIND * SLOTS)

            start_from_own("conv2")
            act.sem_inc(h_copied, 2)
            act.sem_inc(a_copied, 2)
            act.sem_inc(a_stored_early, 16)

            def copy_source(c, k, ps):
                return act.activation(a_rows[:, k], ps.rearrange("p (b f) -> p b f", f=H), ACT.Copy)

            with act.If(is_ordered(act) > 0):
                with act.Fori(0, AHEAD) as c:
                    stage_chunk("conv2", c, D, c * SLOTS + BEHIND * SLOTS)
                    take_root(bass.ds(c * CB, CB), c + 2)
                    act.wait_ge(shift_ready, c + 2)
                    act.sem_inc(normalise_turn, 1)
                    for j in range(CB):
                        last = normalise(c * CB + j, chunk_sums[:, j * D:(j + 1) * D])
                    last.then_inc(rows_ready["edge"], 1)
                    act.wait_ge(rows_turned["edge"], c + 1)
                    act.sem_inc(copy_turn, 1)
                    act.activation(acc[0:D, bass.ds(c * CN, CN)], ps_z[0:D, 1, 0:CN], ACT.Copy)
                    act.activation(chunk_sums[0:D, :], ps_z[0:D, 1, 0:CN], ACT.Copy).then_inc(h_copied, 1)
                    act.wait_ge(a_ready, c + 1)
                    act.wait_ge(a_stored_early, c * 16 + 16)
                    copy_source(c, 0, ps_z[:, 0, :]).then_inc(a_copied, 1)

            def copy_h(c):
                act.wait_ge(rows_turned["edge"], c + 1)
                act.activation(acc[0:D, c * CN:(c + 1) * CN], ps_e[0:D, c % 2, 0:CN], ACT.Copy
                               ).then_inc(h_copied, 1)

            def copy_a(c, chunks, when):
                act.wait_ge(a_ready, c + 1)
                if c - 2 in chunks:
                    act.wait_ge(*stored_chunks(a_stored[when], range(chunks[0], c))[c % 2])
                copy_source(c, c % 2, ps_a[:, c % 2, :]).then_inc(a_copied, 1)

            def source_list(chunks, when):
                if when == "last":
                    wait_first_rows(act)
                end = chunks[-1] + 1
                take_root(slice(chunks[0] * CB, end * CB), end + 1, len(chunks))
                act.wait_ge(shift_ready, end + 1)
                for c in range(chunks[0], end + 2):
                    if c in chunks:
                        for b in range(c * CB, (c + 1) * CB):
                            last = normalise(b)
                        last.then_inc(rows_ready["edge"], 1)
                    if c - 1 in chunks:
                        copy_h(c - 1)
                    if c - 2 in chunks:
                        copy_a(c - 2, chunks, when)
            late_lists(act, source_list)
            act.sem_inc(acc_started["edge"], 2)
            for c in range(CHUNKS):
                act.wait_ge(self_ready, c + 1)
                act.activation(acc[:, c * CN:(c + 1) * CN], ps_z[:, c % 2, :], ACT.Relu,
                               bias=eb1_col[:, 0:1]).then_inc(acc_started["edge"], 1)

            def relu_messages(g, s):
                act.wait_ge(messages_added, g + 2)
                rows = hidden[:, s % 2, 0:tiles(g), :]
                act.activation(rows, rows, ACT.Relu).then_inc(hidden_ready, 1)

            def stage_for_output(c, g):
                act.wait_ge(out_ready, c + 1)
                stage_chunk("edge", c, H, g)
            for_groups(act, relu_messages, {0: stage_for_output})

            def sweep_relu(g, n, j):
                act.wait_ge(sw["edge"]["messages"], n + 1)
                act.activation(hidden[:, 0], hidden[:, 0], ACT.Relu).then_inc(sw["edge"]["hidden"], 1)
            sweep(act, sweep_relu)

        @block.tensor
        def _(pe):
            pe.wait_ge(consts_made, 1)
            for rows, ready, turned, banks in (
                    (rel_rows, rel_ready, rel_turned, [ps_e[:, 0, 0:512], ps_e[:, 0, 512:], ps_e[:, 1, 0:512],
                                                       ps_e[:, 1, 512:]]),
                    (src_f, src_ready, src_turned, [ps_a[:, 0, :], ps_a[:, 1, :], ps_z[:, 0, :], ps_z[:, 1, :]])):
                pe.wait_ge(ready, 1)
                for j in range(2 * GT):
                    last = pe.transpose(banks[j // 4][:, j % 4 * R:(j % 4 + 1) * R],
                                        rows[0:R, j * P:(j + 1) * P], ident[0:R, 0:R])
                last.then_inc(turned, 1)

            def deg_step(q, k):
                pe.wait_ge(deg_hot_ready, q + 1)
                for half, (ps, emptied, per_step, done) in enumerate(((ps_a, deg_added, HG, deg_summed),
                                                                      (ps_z, deg_staged, 1, deg_summed_pool))):
                    pe.wait_ge(emptied, q * per_step + 1)
                    for t in range(HG * GT):
                        g, c = t // GT, t % GT
                        at = half * HG * GT + t
                        last = pe.matmul(ps[0:U, k, g * WU:(g + 1) * WU], lo_hot[:, k, :, at],
                                         hi_hot[:, k, :, at], start=(c == 0), stop=(c == GT - 1))
                    last.then_inc(done, 1)

            pe.wait_ge(src_col_ready, 1)
            with pe.Fori(0, DSTEPS - 1, 2) as i:
                for k in range(2):
                    deg_step(i + k, k)
            deg_step(DSTEPS - 1, 0)

            def sweep_deg(g, n, j):
                pe.wait_ge(sw["deg"]["hot"], n + 1)
                for c in range(GT):
                    last = pe.matmul(ps_a[0:U, 0, 0:WU], lo_hot[:, 0, :, c], hi_hot[:, 0, :, c],
                                     start=(c == 0), stop=(c == GT - 1))
                last.then_inc(sw["deg"]["summed"], 1)
            sweep(pe, sweep_deg)
            pe.wait_ge(pass_done["deg"], 1)
            pe.wait_ge(consts_made, 9)
            for q in range(WU):
                last = pe.matmul(ps_z[:, 0, 0:NB], select[:, q, :],
                                 deg.rearrange("l (b q) -> l q b", q=WU)[:, q, :],
                                 start=(q == 0), stop=(q == WU - 1))
            last.then_inc(deg_turned, 1)

            def turn_rows(p, c, k):
                for j in range(CB):
                    last = pe.transpose(ps_e[0:D, k, j * P:(j + 1) * P], t_sb[:, c * CB + j, :], ident[:, :])
                last.then_inc(rows_turned[p], 1)

            def multiply(p, c, rows, weights):
                if p in CONVS:
                    pe.wait_ge(scaled[p], c + 1)
                elif c >= 2:
                    pe.wait_ge(out_ready, c)
                for j in range(CB):
                    last = pe.matmul(ps_z[:, c % 2, j * D:(j + 1) * D],
                                     acc[0:rows, c * CN + j * P:c * CN + (j + 1) * P], weights,
                                     start=True, stop=True)
                last.then_inc(product_ready[p], 1)

            def multiply_early(p, c, rows, weights, freed, value):
                pe.wait_ge(chunk_staged[p], c + 1)
                pe.wait_ge(freed, value)
                for j in range(CB):
                    last = pe.matmul(ps_z[:, 0, j * D:(j + 1) * D], chunk_sums[0:rows, j * P:(j + 1) * P],
                                     weights, start=True, stop=True)
                last.then_inc(product_ready[p], 1)

            def own_terms(p, c):
                pe.wait_ge(rows_ready[p], c + 1)
                pe.wait_ge(acc_started[p], c + 1)
                turn_rows(p, c, c % 2)

            def sum_group(p, g, s, weights, waits):
                k, n = s % 2, tiles(g)
                for what, value in waits:
                    pe.wait_ge(what, value)
                pe.wait_ge(onehot_ready[p], g + 1)
                pe.wait_ge(added[p], g + 1)
                for c in range(n):
                    lhs = weights(c)
                    last = pe.matmul(ps_a[0:lhs.shape[1], k, 0:W], lhs, onehot[:, k, c, :],
                                     start=(c == 0), stop=(c == n - 1))
                last.then_inc(summed[p], 1)

            def sweep_sum(p, n, weights):
                pe.wait_ge(sw[p]["hot"], n + 1)
                for c in range(GT):
                    lhs = weights(c)
                    last = pe.matmul(ps_a[0:lhs.shape[1], 0, 0:W], lhs, onehot[:, 0, c, :],
                                     start=(c == 0), stop=(c == GT - 1))
                last.then_inc(sw[p]["summed"], 1)

            def conv_sums(p, chunk=None):
                def body(g, s):
                    count = (16 * (GT * (g // SLOTS) + tiles(g)) if isinstance(g, int)
                             else uses(g, s, SLOTS) * (16 * GT) + 16 * GT)
                    sum_group(p, g, s, lambda c: gath[:, s, c, 0:D], [(gathered[p][s], count)])
                for_groups(pe, body, chunk)

                def sweep_conv(g, n, j):
                    pe.wait_ge(sw[p]["gathered"], n * (16 * GT) + 16 * GT)
                    sweep_sum(p, n, lambda c: gath[:, 0, c, 0:D])
                sweep(pe, sweep_conv)
                pe.wait_ge(pass_done[p], 1)

            for c in range(CHUNKS):
                own_terms("conv1", c)
            pe.wait_ge(weights_loaded, 16 * 9)
            conv_sums("conv1", {2: lambda c, g: multiply_early("conv1", c, D, w1_sb[:, :], scaled["conv1"], c + 2)})
            late_chunks(pe, lambda c, k: multiply("conv1", c, D, w1_sb[:, :]))
            for c in range(CHUNKS):
                own_terms("conv2", c)
            def turn_early(c, g):
                pe.wait_ge(rows_ready["edge"], c + 1)
                pe.wait_ge(h_copied, c + 2)
                pe.sem_inc(transpose_turn, 1)
                for j in range(CB):
                    last = pe.transpose(ps_z[0:D, 1, j * P:(j + 1) * P], chunk_sums[:, j * D:(j + 1) * D],
                                        ident[:, :])
                last.then_inc(rows_turned["edge"], 1)

            def table_products(ps, chunk, side, done):
                for j in range(CB):
                    last = pe.matmul(ps[:, j * H:(j + 1) * H], chunk[:, j * P:(j + 1) * P], wab_sb[:, side, :],
                                     start=True, stop=True)
                last.then_inc(done, 1)

            def source_early(c, g):
                pe.wait_ge(h_copied, c + 3)
                pe.wait_ge(scaled["conv2"], c + 3)
                table_products(ps_z[:, 0, :], chunk_sums[0:D, :], 0, a_ready)

            conv_sums("conv2", {1: lambda c, g: multiply_early("conv2", c, D, w2_sb[:, :], a_copied, c + 2),
                                4: turn_early, 6: source_early})

            def turn_chunk(c):
                pe.wait_ge(rows_ready["edge"], c + 1)
                pe.wait_ge(h_copied, c + 1)
                turn_rows("edge", c, c % 2)

            def acc_chunk(c):
                return acc[0:D, c * CN:(c + 1) * CN]

            def source_list(chunks, when):
                if when == "last":
                    pe.wait_ge(h_copied, AHEAD + 2)
                    pe.wait_ge(a_copied, AHEAD + 2)
                for c in chunks:
                    multiply("conv2", c, D, w2_sb[:, :])
                for c in [*chunks, chunks[-1] + 1]:
                    if c in chunks:
                        turn_chunk(c)
                    if c - 1 in chunks:
                        a = c - 1
                        pe.wait_ge(h_copied, a + 3)
                        pe.wait_ge(a_copied, a + 1)
                        table_products(ps_a[:, a % 2, :], acc_chunk(a), 0, a_ready)
            late_lists(pe, source_list)
            pe.wait_ge(scaled["conv2"], CHUNKS + 2)
            for c in range(CHUNKS):
                pe.wait_ge(b_copied, c + 1)
                table_products(ps_z[:, c % 2, :], acc_chunk(c), 1, b_ready)
            pe.sem_inc(expanded, 2)

            def expand(g, s):
                k = s % 2
                pe.wait_ge(onehot_t_ready, g + 1)
                pe.wait_ge(window_loaded[k], (uses(g, s, 2) + 1) * 32)
                if not (isinstance(g, int) and g == 0):
                    pe.wait_ge(messages_added, g)
                for c in range(tiles(g)):
                    last = pe.matmul(ps_e[:, k, c * H:(c + 1) * H], onehot_t[:, k, c * P:(c + 1) * P],
                                     b_win[:, k, :], start=True, stop=True)
                last.then_inc(expanded, 1)

            pe.wait_ge(b_copied, CHUNKS + 2)
            pe.wait_ge(wself_ready, 1)
            for c in range(CHUNKS):
                if c in (EARLY, EARLY + 1):
                    expand(c - EARLY, c - EARLY)
                pe.wait_ge(acc_started["edge"], c + 1)
                pe.matmul(ps_z[:, c % 2, :], wself_sb[:, :], acc[0:D, c * CN:(c + 1) * CN],
                          start=True, stop=True).then_inc(self_ready, 1)
            pe.wait_ge(acc_started["edge"], CHUNKS + 2)

            def edge_group(g, s):
                sum_group("edge", g, s, lambda c: hidden[:, s % 2, c, :], [(hidden_ready, g + 1)])
                if not (isinstance(g, int) and g + 2 >= G):
                    expand(g + 2, (s + 2) % SLOTS)
            for_groups(pe, edge_group,
                       {2: lambda c, g: multiply_early("edge", c, H, ew2_sb[:, :], out_ready, c + 1)})

            def sweep_edge(g, n, j):
                s = sw["edge"]
                pe.wait_ge(s["loaded"], n * 32 + 32)
                pe.wait_ge(s["hot_t"], n + 1)
                for c in range(GT):
                    last = pe.matmul(ps_e[:, 0, c * H:(c + 1) * H], onehot_t[:, 0, c * P:(c + 1) * P],
                                     b_win[:, 0, :], start=True, stop=True)
                last.then_inc(s["expanded"], 1)
                pe.wait_ge(s["hidden"], n + 1)
                sweep_sum("edge", n, lambda c: hidden[:, 0, c, :])
            sweep(pe, sweep_edge)
            pe.wait_ge(pass_done["edge"], 1)
            late_chunks(pe, lambda c, k: multiply("edge", c, H, ew2_sb[:, :]))


_INS = ["x", "src", "dst", "L0_gnn_W1", "L0_gnn_b1", "L0_gnn_W2", "L0_gnn_b2",
        "L1_gnn_W1", "L1_gnn_b1", "L1_gnn_W2", "L1_gnn_b2"]


def kernel(**inputs):
    import numpy as np
    import concourse.bacc as bacc
    from concourse.bass_utils import run_bass_kernel_spmd

    nc = bacc.Bacc("TRN2", target_bir_lowering=False, num_devices=1)
    arrays, args = {}, []
    for name in _INS:
        a = np.ascontiguousarray(inputs[name])
        arrays[f"in_{name}"] = a
        args.append(nc.dram_tensor(f"in_{name}", a.shape, mybir.dt.from_np(a.dtype), kind="ExternalInput").ap())
    out = nc.dram_tensor("out_0", inputs["x"].shape, F32, kind="ExternalOutput").ap()
    gnn_program(nc, *args, out)
    r = run_bass_kernel_spmd(nc, [arrays], core_ids=[0])
    return r.results[0]["out_0"]
```
